# Optimizing a Trainium2 kernel written in Bass

```python
import numpy as np
import jax
import jax.numpy as jnp

def _softmax(x, axis=-1):
    return jax.nn.softmax(x, axis=axis)

def _gelu(x):
    return jax.nn.gelu(x, approximate=True)

def _silu(x):
    return jax.nn.silu(x)

def _sigmoid(x):
    return jax.nn.sigmoid(x)

def _layernorm(x, axis=-1, eps=1e-05):
    m = jnp.mean(x, axis=axis, keepdims=True)
    v = jnp.var(x, axis=axis, keepdims=True)
    return (x - m) / jnp.sqrt(v + eps)

def _scatter_add(tgt, idx, src, axis=0):
    return tgt.at[idx].add(src)

def _segment_sum(src, seg, n):
    return jax.ops.segment_sum(src, seg, n)
kernel_name = 'mk_adaln_ffn_d1_seqx_r4_1088e7'

def setup_inputs(seed: int=0):
    np.random.seed(seed)
    _w = jnp.asarray

    def _rec_inputs():
        import jax
        import jax.numpy as jnp
        _rk = jax.random.key(seed)
        x = -7.109e-05 + 0.9999 * jax.random.normal(jax.random.fold_in(_rk, 1), (64, 64, 512), jnp.float32)
        _lenS = 64 - jax.random.randint(jax.random.fold_in(_rk, 7), (64,), 0, max(1, 64 // 4) + 1, jnp.int32)
        _lenS2 = 64 - jax.random.randint(jax.random.fold_in(_rk, 8), (64,), 0, max(1, 64 // 4) + 1, jnp.int32)
        itok_B_0_7 = jax.random.randint(jax.random.fold_in(_rk, 11), (64,), 0, 8, jnp.int32)
        return (x, itok_B_0_7)
    x, itok_B_0_7 = _rec_inputs()

    def _L0_cond_setup():
        import jax, jax.numpy as jnp
        import numpy as np
        B, C, D, T, N_SUBJECTS = (128, 64, 64, 512, 8)
        key = jax.random.key(seed)
        kx, ks, kw = jax.random.split(key, 3)
        x = jax.random.normal(kx, (B, C, T), dtype=jnp.float32)
        subjects = jax.random.randint(ks, (B,), 0, N_SUBJECTS, dtype=jnp.int64)
        weights = jax.random.normal(kw, (N_SUBJECTS, C, D), dtype=jnp.float32) * (1.0 / C ** 0.5)
        return {'x': x, 'subjects': subjects, 'weights': weights}
    _L0_cond_all = _L0_cond_setup()
    _L0_cond_in = {k: v for k, v in _L0_cond_all.items() if k in ('weights',)}
    del _L0_cond_all

    def _L0_ffn_setup():
        import jax, jax.numpy as jnp
        import numpy as np
        B, T, C = (2, 256, 512)
        E, TOPK = (8, 2)
        F_MOE = 352
        F_SHARED = 1408
        key = jax.random.key(seed)
        ks = jax.random.split(key, 9)
        s = 0.02
        return {'x': jax.random.normal(ks[0], (B, T, C), dtype=jnp.float32), 'gate_w': jax.random.normal(ks[1], (E, C), dtype=jnp.float32) * s, 'expert_fc1': jax.random.normal(ks[2], (E, F_MOE, C), dtype=jnp.float32) * s, 'expert_fc2': jax.random.normal(ks[3], (E, F_MOE, C), dtype=jnp.float32) * s, 'expert_proj': jax.random.normal(ks[4], (E, C, F_MOE), dtype=jnp.float32) * s, 'shared_fc1': jax.random.normal(ks[5], (F_SHARED, C), dtype=jnp.float32) * s, 'shared_fc2': jax.random.normal(ks[6], (F_SHARED, C), dtype=jnp.float32) * s, 'shared_proj': jax.random.normal(ks[7], (C, F_SHARED), dtype=jnp.float32) * s, 'shared_gate_w': jax.random.normal(ks[8], (1, C), dtype=jnp.float32) * s}
    _L0_ffn_all = _L0_ffn_setup()
    _L0_ffn_in = {k: v for k, v in _L0_ffn_all.items() if k in ('gate_w', 'expert_fc1', 'expert_fc2', 'expert_proj', 'shared_fc1', 'shared_fc2', 'shared_proj', 'shared_gate_w')}
    del _L0_ffn_all
    return {'x': x, 'itok_B_0_7': itok_B_0_7, 'L0_cond_weights': _L0_cond_in['weights'], 'L0_ffn_gate_w': _L0_ffn_in['gate_w'], 'L0_ffn_expert_fc1': _L0_ffn_in['expert_fc1'], 'L0_ffn_expert_fc2': _L0_ffn_in['expert_fc2'], 'L0_ffn_expert_proj': _L0_ffn_in['expert_proj'], 'L0_ffn_shared_fc1': _L0_ffn_in['shared_fc1'], 'L0_ffn_shared_fc2': _L0_ffn_in['shared_fc2'], 'L0_ffn_shared_proj': _L0_ffn_in['shared_proj'], 'L0_ffn_shared_gate_w': _L0_ffn_in['shared_gate_w']}

def reference(x, itok_B_0_7, L0_cond_weights, L0_ffn_gate_w, L0_ffn_expert_fc1, L0_ffn_expert_fc2, L0_ffn_expert_proj, L0_ffn_shared_fc1, L0_ffn_shared_fc2, L0_ffn_shared_proj, L0_ffn_shared_gate_w):
    import jax
    import jax.numpy as jnp

    def _L0_cond_ref(x, subjects, weights):
        import jax, jax.numpy as jnp
        import numpy as np
        B, C, D, T, N_SUBJECTS = (128, 64, 64, 512, 8)
        w = weights[subjects]
        out = jnp.einsum('bct,bcd->bdt', x, w)
        return out

    def _L0_ffn_ref(x, gate_w, expert_fc1, expert_fc2, expert_proj, shared_fc1, shared_fc2, shared_proj, shared_gate_w):
        import jax, jax.numpy as jnp
        import numpy as np
        B, T, C = (2, 256, 512)
        E, TOPK = (8, 2)
        F_MOE = 352
        F_SHARED = 1408
        b, t, c = x.shape
        xf = x.reshape(-1, c)
        n = xf.shape[0]
        router = xf @ gate_w.T
        probs = jax.nn.softmax(router.astype(jnp.float32), axis=1).astype(x.dtype)
        top_p, top_i = jax.lax.top_k(probs, TOPK)
        combine = jnp.zeros((n, E), dtype=x.dtype).at[jnp.arange(n)[:, None], top_i].set(top_p)
        h1 = jnp.einsum('nc,efc->enf', xf, expert_fc1)
        h2 = jnp.einsum('nc,efc->enf', xf, expert_fc2)
        h = jax.nn.silu(h1) * h2
        out_e = jnp.einsum('enf,ecf->enc', h, expert_proj)
        y = jnp.einsum('ne,enc->nc', combine, out_e)
        s1 = xf @ shared_fc1.T
        s2 = xf @ shared_fc2.T
        shared = jax.nn.silu(s1) * s2 @ shared_proj.T
        y = y + jax.nn.sigmoid(xf @ shared_gate_w.T) * shared
        return y.reshape(b, t, c)
    x = x + _L0_ffn_ref(_L0_cond_ref(x, itok_B_0_7, L0_cond_weights), L0_ffn_gate_w, L0_ffn_expert_fc1, L0_ffn_expert_fc2, L0_ffn_expert_proj, L0_ffn_shared_fc1, L0_ffn_shared_fc2, L0_ffn_shared_proj, L0_ffn_shared_gate_w)
    return x

_drawn_inputs = setup_inputs


def setup_inputs(seed=0):
    import zlib

    import numpy as np

    out = dict(_drawn_inputs(seed))
    spreads = {}
    factors = {'L0_ffn_gate_w': 5.361,
     'L0_ffn_expert_fc1': 4.699,
     'L0_ffn_expert_fc2': 4.601,
     'L0_ffn_expert_proj': 4.605,
     'L0_ffn_shared_gate_w': 44.834,
     'L0_ffn_shared_fc1': 4.336,
     'L0_ffn_shared_fc2': 4.24,
     'L0_ffn_shared_proj': 4.239}
    for name, (base, spread) in spreads.items():
        noise = np.random.default_rng([zlib.crc32(name.encode()), seed]).standard_normal(out[name].shape)
        drawn = base * np.exp(spread * noise) if base else spread * noise
        out[name] = jnp.asarray(drawn.astype(out[name].dtype))
    for name, factor in factors.items():
        out[name] = (out[name] * factor).astype(out[name].dtype)
    return out
```

```python
from contextlib import ExitStack

import concourse.bass as bass
from concourse import mybir

ALU = mybir.AluOpType
ACT = mybir.ActivationFunctionType
AX_X = mybir.AxisListType.X
F32 = mybir.dt.float32
F32R = mybir.dt.float32r
BF16 = mybir.dt.bfloat16
I32 = mybir.dt.int32
U32 = mybir.dt.uint32

P = 128
BATCH, CIN, C = 64, 64, 512
DOUT = 64
NSUB = 8
TOKENS = BATCH * DOUT
TILES = TOKENS // P
KC = C // P
E = 8
F = 352
FCH = [(0, 128), (128, 128), (256, 96)]
FS = 1408
SCH = FS // P
PARTS = [list(range(0, 5)), list(range(5, 11))]
BT = 4
BLOCKS = TILES // BT
BN = BT * P
TS = 256
XT = 2 * TOKENS // TS + E - 1
HALVES = 2 * XT
CHOICES = 2 * TILES
GRP = 16
THR = TOKENS // TS
BIG = -3.0e38

CONST = {}
_at = 0
for _name, _n in (("ident", P), ("before", P), ("rev", E * TILES), ("col", P), ("pidx", 1),
                  ("choice_tile", CHOICES), ("thr", THR), ("xtile", XT)):
    CONST[_name] = (_at, _n)
    _at += _n
NCONST = _at


def build_program(nc, x, subj, cond_w, gates, ew12, ewp, sw12, swp, consts, out):
    xf_dram = nc.dram_tensor("xf_rows", (TOKENS, C), F32, kind="Internal").ap()
    part_dram = nc.dram_tensor("partial_rows", (TOKENS, C), F32, kind="Internal").ap()
    slot_dram = nc.dram_tensor("slot_rows", (XT * TS, C), F32, kind="Internal").ap()
    x_rows = x.rearrange("b j t -> (b j) t")
    out_rows = out.rearrange("b j t -> (b j) t")

    ctx = ExitStack()
    with ctx:
        def sb(name, shape, dt):
            return ctx.enter_context(nc.sbuf_tensor(name, shape, dt))

        def sem(name):
            return ctx.enter_context(nc.semaphore(name))

        cst = sb("cst", [P, NCONST], F32)
        gate_w = sb("gate_w", [P, KC, E + 1], F32)
        subj_sb = sb("subj_sb", [1, BATCH], I32)
        before_bf = sb("before_bf", [P, P], BF16)
        ones_bf = sb("ones_bf", [P, P], BF16)
        col_bf = sb("col_bf", [P, P], BF16)
        ctile_bf = sb("ctile_bf", [P, CHOICES], BF16)
        logits = sb("logits", [P, E + 1, TILES], F32)
        s_gate = sb("s_gate", [P, TILES], F32)
        p_top = sb("p_top", [P, 2, TILES], F32)
        slot_of = sb("slot_of", [P, 2, TILES], I32)
        token_of = sb("token_of", [P, HALVES], I32)
        tile_expert = sb("tile_expert", [1, XT], I32)
        idx_stage = sb("idx_stage", [P, 4], I32)
        wblk = sb("wblk", [P, 4, P], F32)
        rows = sb("rows", [P, 4, C], F32)
        res = sb("res", [P, 4, C], F32)
        x_hi = sb("x_hi", [P, KC, BN], F32R)
        x_lo = sb("x_lo", [P, KC, BN], F32R)
        w12_hi = sb("w12_hi", [P, 6144], F32R)
        w12_lo = sb("w12_lo", [P, 6144], F32R)
        wp_hi = sb("wp_hi", [P, 3072], F32R)
        wp_lo = sb("wp_lo", [P, 3072], F32R)
        h_hi = sb("h_hi", [P, 6, BN], F32R)
        h_lo = sb("h_lo", [P, 6, BN], F32R)
        raw12 = sb("raw12", [P, 5632], F32)
        rawp = sb("rawp", [P, 3072], F32)
        g_sb = sb("g_sb", [P, 1024], F32)
        h_sb = sb("h_sb", [P, 1024], F32)
        picked = sb("picked", [P, 2, 2, C], F32)
        xt = g_sb[:, :].rearrange("p (s k t) -> p s k t", s=2, k=KC)
        top1 = sb("top1", [P, E, TILES], F32)
        top2 = sb("top2", [P, E, TILES], F32)
        tmp = sb("tmp", [P, E, TILES], F32)
        rest = sb("rest", [P, E, TILES], F32)
        both_bf = sb("both_bf", [P, E, TILES], BF16)
        total = sb("total", [P, E, TILES], F32)
        scan = sb("scan", [P, E, TILES], F32)
        small = sb("small", [P, 8, TILES], F32)
        cmp_thr = sb("cmp_thr", [P, E, THR], F32)
        percnt = sb("percnt", [P, 8, E], F32)
        cmp_tile = sb("cmp_tile", [1, XT, E - 1], F32)
        te_f = sb("te_f", [1, XT], F32)
        posf = sb("posf", [P, CHOICES], F32)
        hi_i = sb("hi_i", [P, CHOICES], I32)
        lo_i = sb("lo_i", [P, CHOICES], I32)
        half_bf = sb("half_bf", [P, CHOICES], BF16)
        lane_bf = sb("lane_bf", [P, CHOICES], BF16)
        pick_bf = picked[:, :, :, :].rearrange("p a b c -> p (a b c)").bitcast(BF16)
        is_lane = pick_bf[:, 0:GRP * P].rearrange("p (g n) -> p g n", g=GRP)
        is_half = pick_bf[:, GRP * P:GRP * (P + HALVES)].rearrange("p (g n) -> p g n", g=GRP)
        ids_bf = sb("ids_bf", [P, GRP, 2, HALVES], BF16)
        tok_f = sb("tok_f", [P, HALVES], F32)

        def const(name, parts=P):
            a, n = CONST[name]
            return cst[0:parts, a:a + n]

        ident = const("ident")

        bank_t = [ctx.enter_context(nc.psum_tensor(f"bank_t{i}", [P, 512], F32)) for i in range(2)]
        bank_o = [ctx.enter_context(nc.psum_tensor(f"bank_o{i}", [P, 512], F32)) for i in range(2)]
        bank_h = [ctx.enter_context(nc.psum_tensor(f"bank_h{i}", [P, 512], F32)) for i in range(4)]

        consts_in = sem("consts_in")
        consts_made = sem("consts_made")
        fx_loaded = [sem(f"fx_loaded{i}") for i in range(4)]
        fw_loaded = [sem(f"fw_loaded{i}") for i in range(4)]
        cond_done = sem("cond_done")
        frow_ready = sem("frow_ready")
        frow_stored = [sem(f"frow_stored{i}") for i in range(4)]
        ft_done = sem("ft_done")
        fxt_ready = sem("fxt_ready")
        routed = sem("routed")
        logits_kept = sem("logits_kept")
        dve_step = sem("dve_step")
        shifted = sem("shifted")
        exps = sem("exps")
        gate_ready = sem("gate_ready")
        both_ready = sem("both_ready")
        ranks_done = sem("ranks_done")
        ids_ready = sem("ids_ready")
        ids_used = sem("ids_used")
        routing_done = sem("routing_done")

        class Ffn:

            def __init__(self, n):
                self.raw_loaded = [sem(f"{n}_raw{i}") for i in range(6)]
                self.w_hi = sem(f"{n}_w_hi")
                self.w_lo = sem(f"{n}_w_lo")
                self.rows_loaded = [sem(f"{n}_rows{i}") for i in range(2)]
                self.t_done = sem(f"{n}_t_done")
                self.x_hi = sem(f"{n}_x_hi")
                self.x_lo = sem(f"{n}_x_lo")
                self.h_full = sem(f"{n}_h_full")
                self.g_ready = sem(f"{n}_g_ready")
                self.h_mul = sem(f"{n}_h_mul")
                self.h_hi = sem(f"{n}_h_hi")
                self.h_lo = sem(f"{n}_h_lo")
                self.o_full = sem(f"{n}_o_full")
                self.o_kept = sem(f"{n}_o_kept")

        shared = [Ffn("s0"), Ffn("s1")]
        ex = Ffn("ex")
        res_loaded = [sem("res_loaded0"), sem("res_loaded1")]
        res_stored = [sem("res_stored0"), sem("res_stored1")]
        y_stored = [sem("y_stored0"), sem("y_stored1")]
        picked_in = [sem("picked_in0"), sem("picked_in1")]
        pick_half = sem("pick_half")
        picked_used = sem("picked_used")
        row_summed = [shared[0].o_kept, picked_used]

        def at_least(eng, s, value):
            if not isinstance(value, int) or value > 0:
                eng.wait_ge(s, value)

        def all_xf_stored(eng):
            for u in range(4):
                eng.wait_ge(frow_stored[u], 16 * (TILES // 4))

        def all_y_stored(eng):
            for u in range(2):
                eng.wait_ge(y_stored[u], 16 * ((XT + 1 - u) // 2))

        def shared_pieces(n):
            for k in range(len(PARTS[n])):
                yield (raw12[:, (k % 5) * 1024:(k % 5 + 1) * 1024], w12_hi[:, k * 1024:(k + 1) * 1024],
                       w12_lo[:, k * 1024:(k + 1) * 1024])
                yield (rawp[:, k * 512:(k + 1) * 512], wp_hi[:, k * 512:(k + 1) * 512],
                       wp_lo[:, k * 512:(k + 1) * 512])

        def expert_pieces(u):
            for k in range(KC):
                a = u * 2816 + k * 2 * F
                yield raw12[:, a:a + 2 * F], w12_hi[:, a:a + 2 * F], w12_lo[:, a:a + 2 * F]
            for k, (_, n) in enumerate(FCH):
                a = u * 1536 + k * 512
                yield rawp[0:n, a:a + 512], wp_hi[0:n, a:a + 512], wp_lo[0:n, a:a + 512]

        PIECES = KC + len(FCH)

        block = ctx.enter_context(nc.Block())

        @block.sync
        def _(sp):
            sp.dma_start(cst[:, :], consts).then_inc(consts_in, 16)
            sp.dma_start(gate_w[:, :, :], gates).then_inc(consts_in, 16)
            sp.dma_start(subj_sb[:, :], subj).then_inc(consts_in, 16)
            sp.wait_ge(consts_in, 48)
            sp.wait_ge(consts_made, 1)

            def front_load(t, u):
                sp.dma_start(res[:, u, :], x_rows[bass.ds(t * P, P), :]).then_inc(fx_loaded[u], 16)
                for k in range(2):
                    s = sp.value_load(subj_sb[0:1, bass.ds(2 * t + k, 1)], min_val=0, max_val=NSUB - 1)
                    sp.dma_start(wblk[64 * k:64 * k + 64, u, 64 * k:64 * k + 64],
                                 cond_w[bass.ds(s, 1), :, :].rearrange("s c d -> (s c) d")).then_inc(fw_loaded[u], 16)

            def front_store(t, u):
                sp.wait_ge(frow_ready, t + 1)
                sp.dma_start(xf_dram[bass.ds(t * P, P), :], rows[:, u, :]).then_inc(frow_stored[u], 16)

            for t in range(4):
                front_load(t, t)
            with sp.Fori(0, TILES // 4 - 1) as it:
                for u in range(4):
                    sp.wait_ge(cond_done, 4 * it + u + 1)
                    front_load(4 * it + u + 4, u)
                    front_store(4 * it + u, u)
            for t in range(TILES - 4, TILES):
                front_store(t, t % 4)

            def shared_pass(n):
                f, src = shared[n], (x_rows, part_dram)[n]
                dst = (part_dram, out_rows)[n]
                if n == 1:
                    sp.wait_ge(ex.w_lo, PIECES * XT)
                for k, ch in enumerate(PARTS[n]):
                    if k >= 5:
                        sp.wait_ge(f.w_lo, 2 * (k - 5) + 1)
                    sp.dma_start(raw12[:, (k % 5) * 1024:(k % 5 + 1) * 1024], sw12[ch]).then_inc(f.raw_loaded[k], 16)
                    sp.dma_start(rawp[:, k * 512:(k + 1) * 512], swp[ch]).then_inc(f.raw_loaded[k], 16)

                def load_rows(b):
                    sp.dma_start(rows[:, :, :], xf_dram[bass.ds(b * BN, BN), :].rearrange("(r p) c -> p r c", p=P)
                                 ).then_inc(f.rows_loaded[0], 16)

                def load_res(b):
                    sp.dma_start(res[:, :, :], src[bass.ds(b * BN, BN), :].rearrange("(r p) c -> p r c", p=P)
                                 ).then_inc(res_loaded[n], 16)

                def store_res(b):
                    sp.wait_ge(row_summed[n], BT * (b + 1))
                    sp.dma_start(dst[bass.ds(b * BN, BN), :].rearrange("(r p) c -> p r c", p=P), res[:, :, :]
                                 ).then_inc(res_stored[n], 16)

                if n == 0:
                    all_xf_stored(sp)
                    sp.wait_ge(ft_done, TILES)
                else:
                    sp.wait_ge(ex.t_done, 2 * XT)
                load_rows(0)
                if n == 0:
                    sp.wait_ge(cond_done, TILES)
                else:
                    all_y_stored(sp)
                load_res(0)
                with sp.Fori(0, BLOCKS - 1) as b:
                    sp.wait_ge(f.t_done, BT * (b + 1))
                    load_rows(b + 1)
                    store_res(b)
                    sp.wait_ge(res_stored[n], 16 * (b + 1))
                    load_res(b + 1)
                store_res(BLOCKS - 1)
                sp.wait_ge(res_stored[n], 16 * BLOCKS)

            shared_pass(0)

            def load_expert(i, u):
                e = sp.value_load(tile_expert[0:1, bass.ds(i, 1)], min_val=0, max_val=E - 1)
                sp.dma_start(raw12[:, u * 2816:(u + 1) * 2816], ew12[bass.ds(e, 1), :, :].rearrange("e p n -> (e p) n")
                             ).then_inc(ex.raw_loaded[u], 16)
                w = ewp[bass.ds(e, 1), :, :].rearrange("e f c -> (e f) c")
                sp.dma_start(rawp[:, u * 1536:u * 1536 + 1024].rearrange("p (k c) -> p k c", k=2),
                             w[0:256, :].rearrange("(k p) c -> p k c", p=P)).then_inc(ex.raw_loaded[u], 16)
                sp.dma_start(rawp[0:96, u * 1536 + 1024:(u + 1) * 1536], w[256:F, :]).then_inc(ex.raw_loaded[u], 16)

            def store_y(i, u):
                sp.wait_ge(ex.o_kept, 2 * (i + 1))
                sp.dma_start(slot_dram[bass.ds(i * TS, TS), :].rearrange("(r p) c -> p r c", p=P),
                             res[:, 2 * u:2 * u + 2, :]).then_inc(y_stored[u], 16)

            sp.wait_ge(routing_done, 1)
            load_expert(0, 0)
            load_expert(1, 1)

            def expert_step(i, u, last):
                if not last:
                    sp.wait_ge(ex.w_lo, PIECES * (i + 1))
                    load_expert(i + 2, u)
                store_y(i, u)

            with sp.Fori(0, (XT - 3) // 2) as it:
                for u in range(2):
                    expert_step(2 * it + u, u, False)
            for i in range(XT - 3, XT):
                expert_step(i, i % 2, i + 2 >= XT)

            shared_pass(1)

        @block.gpsimd
        def _(pool):
            nc.gpsimd.memset(wblk[:, :, :], 0.0).then_inc(consts_made, 1)
            pool.wait_ge(routing_done, 1)
            pool.wait_ge(shared[0].t_done, TILES)

            def gather_rows(i, u):
                at_least(pool, ex.t_done, 2 * i - 2)
                nc.gpsimd.tensor_copy(idx_stage[:, 2 * u:2 * u + 2], token_of[:, bass.ds(2 * i, 2)])
                pool.drain()
                for r in range(2):
                    s = 2 * u + r
                    pool.indirect_dma_start(rows[:, s, :], None, xf_dram,
                                            bass.IndirectOffsetOnAxis(idx_stage[:, s:s + 1].bitcast(U32), 0),
                                            ).then_inc(ex.rows_loaded[u], 16)

            gather_rows(0, 0)
            gather_rows(1, 1)
            with pool.Fori(1, (XT - 1) // 2) as it:
                for u in range(2):
                    gather_rows(2 * it + u, u)
            gather_rows(XT - 1, 0)

            all_y_stored(pool)

            def gather_slots(t, u):
                at_least(pool, picked_used, t - 1)
                nc.gpsimd.tensor_copy(idx_stage[:, 2 * u:2 * u + 2], slot_of[:, :, bass.ds(t, 1)].rearrange("p a b -> p (a b)"))
                pool.drain()
                for k in range(2):
                    pool.indirect_dma_start(picked[:, u, k, :], None, slot_dram,
                                            bass.IndirectOffsetOnAxis(idx_stage[:, 2 * u + k:2 * u + k + 1].bitcast(U32), 0),
                                            ).then_inc(picked_in[u], 16)

            pool.wait_ge(ex.rows_loaded[0], 32 * ((XT + 1) // 2))
            gather_slots(0, 0)
            gather_slots(1, 1)
            with pool.Fori(1, TILES // 2) as it:
                for u in range(2):
                    gather_slots(2 * it + u, u)

        @block.tensor
        def _(pe):
            pe.wait_ge(consts_in, 48)

            def front_map(t, it, u):
                pe.wait_ge(fx_loaded[u], 16 * (it + 1))
                pe.wait_ge(fw_loaded[u], 32 * (it + 1))
                at_least(pe, frow_ready, t - 1)
                pe.matmul(bank_h[u % 2][:, :], wblk[:, u, :], res[:, u, :], start=True, stop=True).then_inc(cond_done, 1)

            def front_transpose(t, u):
                pe.wait_ge(frow_ready, t + 1)
                at_least(pe, fxt_ready, t - 1)
                for k in range(KC):
                    m = pe.transpose(bank_t[u % 2][:, k * P:(k + 1) * P], rows[:, u, k * P:(k + 1) * P], ident)
                m.then_inc(ft_done, 1)

            def front_route(t, u):
                pe.wait_ge(fxt_ready, t + 1)
                at_least(pe, logits_kept, t - 1)
                for k in range(KC):
                    m = pe.matmul(bank_o[u % 2][:, 0:E + 1], xt[:, u % 2, k, :], gate_w[:, k, :],
                                  start=(k == 0), stop=(k == KC - 1))
                m.then_inc(routed, 1)

            for t in range(4):
                front_map(t, 0, t)
                if t >= 1:
                    front_transpose(t - 1, t - 1)
                if t >= 2:
                    front_route(t - 2, t - 2)
            with pe.Fori(1, TILES // 4) as it:
                for u in range(4):
                    front_map(4 * it + u, it, u)
                    front_transpose(4 * it + u - 1, (u - 1) % 4)
                    front_route(4 * it + u - 2, (u - 2) % 4)
            front_transpose(TILES - 1, 3)
            front_route(TILES - 2, 2)
            front_route(TILES - 1, 3)

            both = both_bf[:, :, :].rearrange("p e t -> p (e t)")
            pe.wait_ge(both_ready, 1)
            pe.wait_ge(logits_kept, TILES)
            pe.matmul(bank_o[0][:, 0:E * TILES], before_bf[:, :], both, start=True, stop=True)
            pe.matmul(bank_o[1][:, 0:E * TILES], ones_bf[:, :], both, start=True, stop=True).then_inc(ranks_done, 1)
            for g in range(CHOICES // GRP):
                pe.wait_ge(ids_ready, g + 1)
                for j in range(GRP):
                    m = pe.matmul(bank_t[0][:, 0:2 * HALVES], is_lane[:, j, :],
                                  ids_bf[:, j, :, :].rearrange("p a b -> p (a b)"),
                                  start=(g == 0 and j == 0), stop=(g == CHOICES // GRP - 1 and j == GRP - 1))
                m.then_inc(ids_used, 1)

            def transposes(f, n, slots, loaded):
                pe.wait_ge(*loaded)
                for r, s in enumerate(slots):
                    at_least(pe, f.x_lo, n + r - 1)
                    for k in range(KC):
                        m = pe.transpose(bank_t[r % 2][:, k * P:(k + 1) * P], rows[:, s, k * P:(k + 1) * P], ident)
                    m.then_inc(f.t_done, 1)

            def product(dst, stat, moving, first, last):
                (sh, sl), (mh, ml) = stat, moving
                pe.matmul(dst, sh, mh, start=first, stop=False)
                pe.matmul(dst, sh, ml, start=False, stop=False)
                return pe.matmul(dst, sl, mh, start=False, stop=last)

            def shared_pass(n):
                f, chunks = shared[n], len(PARTS[n])

                def stage1(b):
                    pe.wait_ge(f.x_lo, BT * (b + 1))
                    for j in range(chunks):
                        pe.wait_ge(f.w_lo, 2 * j + 1)
                        last = max(q for q in range(-2, j) if q % chunks % 2 == j % 2)
                        at_least(pe, f.h_mul, b * chunks + last + 1)
                        for h in range(2):
                            for k in range(KC):
                                a = j * 1024 + k * 256 + h * P
                                m = product(bank_h[2 * (j % 2) + h][:, :], (w12_hi[:, a:a + P], w12_lo[:, a:a + P]),
                                            (x_hi[:, k, :], x_lo[:, k, :]), k == 0, k == KC - 1)
                        m.then_inc(f.h_full, 1)

                def stage2(b):
                    for r in range(BT):
                        at_least(pe, f.o_kept, b * BT + r - 1)
                        for j in range(chunks):
                            if r == 0:
                                pe.wait_ge(f.h_lo, b * chunks + j + 1)
                            c = slice(r * P, (r + 1) * P)
                            w = slice(j * 512, (j + 1) * 512)
                            pe.wait_ge(f.w_lo, 2 * j + 2)
                            m = product(bank_o[r % 2][:, :], (h_hi[:, j, c], h_lo[:, j, c]),
                                        (wp_hi[:, w], wp_lo[:, w]), j == 0, j == chunks - 1)
                        m.then_inc(f.o_full, 1)

                transposes(f, 0, range(BT), (f.rows_loaded[0], 16))

                def step(b):
                    stage1(b)
                    transposes(f, (b + 1) * BT, range(BT), (f.rows_loaded[0], 16 * (b + 2)))
                    stage2(b)

                step(0)
                with pe.Fori(1, BLOCKS - 1) as b:
                    step(b)
                stage1(BLOCKS - 1)
                stage2(BLOCKS - 1)

            pe.wait_ge(routing_done, 1)
            shared_pass(0)

            def expert_stage1(i, u):
                pe.wait_ge(ex.x_lo, 2 * (i + 1))
                pe.wait_ge(ex.w_lo, PIECES * i + KC)
                for j, (f0, fn) in enumerate(FCH):
                    at_least(pe, ex.h_mul, 3 * (i - 1) + j + 1)
                    for h in range(2):
                        for k in range(KC):
                            a = u * 2816 + k * 2 * F + h * F + f0
                            m = product(bank_h[j][0:fn, h * TS:(h + 1) * TS], (w12_hi[:, a:a + fn], w12_lo[:, a:a + fn]),
                                        (x_hi[:, k, 0:TS], x_lo[:, k, 0:TS]), k == 0, k == KC - 1)
                    m.then_inc(ex.h_full, 1)

            def expert_stage2(i, u):
                pe.wait_ge(ex.w_lo, PIECES * (i + 1))
                at_least(pe, ex.o_kept, 2 * i)
                for ks in ((0, 1), (2,)):
                    pe.wait_ge(ex.h_lo, 3 * i + ks[-1] + 1)
                    for r in range(2):
                        c = slice(r * P, (r + 1) * P)
                        for k in ks:
                            fn = FCH[k][1]
                            w = slice(u * 1536 + k * 512, u * 1536 + (k + 1) * 512)
                            m = product(bank_o[r][:, :], (h_hi[0:fn, k, c], h_lo[0:fn, k, c]),
                                        (wp_hi[0:fn, w], wp_lo[0:fn, w]), k == 0, k == 2)
                        if ks == (2,):
                            m.then_inc(ex.o_full, 1)

            pe.wait_ge(shared[0].o_kept, TILES)
            transposes(ex, 0, (0, 1), (ex.rows_loaded[0], 32))

            def expert_step(i, it, u):
                expert_stage1(i, u)
                transposes(ex, 2 * (i + 1), (2 * (1 - u), 2 * (1 - u) + 1), (ex.rows_loaded[1 - u], 32 * (it + 1 + u)))
                expert_stage2(i, u)

            for u in range(2):
                expert_step(u, 0, u)
            with pe.Fori(1, (XT - 1) // 2) as it:
                for u in range(2):
                    expert_step(2 * it + u, it, u)
            expert_stage1(XT - 1, 0)
            expert_stage2(XT - 1, 0)

            pe.wait_ge(ex.o_kept, 2 * XT)
            shared_pass(1)

        @block.scalar
        def _(act):
            copy = lambda o, i: nc.scalar.activation(o, i, ACT.Copy)

            def front_rows(t, u, waits):
                act.wait_ge(cond_done, t + 1)
                if waits is not None:
                    act.wait_ge(frow_stored[u], 16 * waits)
                    act.wait_ge(ft_done, t - 3)
                copy(rows[:, u, :], bank_h[u % 2][:, :]).then_inc(frow_ready, 1)

            for t in range(4):
                front_rows(t, t, None)
            with act.Fori(1, TILES // 4) as it:
                for u in range(4):
                    front_rows(4 * it + u, u, it)

            act.wait_ge(shifted, 1)
            nc.scalar.activation(tmp[:, :, :], tmp[:, :, :], ACT.Exp).then_inc(exps, 1)
            nc.scalar.activation(small[:, 2, :], small[:, 2, :], ACT.Exp).then_inc(exps, 1)
            act.wait_ge(logits_kept, TILES)
            nc.scalar.activation(s_gate[:, :], logits[:, E, :], ACT.Sigmoid).then_inc(gate_ready, 1)

            def shared_pass(n):
                f, chunks = shared[n], len(PARTS[n])
                if n == 1:
                    act.wait_ge(ex.o_full, 2 * XT)
                for k, (raw, hi, _) in enumerate(shared_pieces(n)):
                    act.wait_ge(f.raw_loaded[k // 2], 32)
                    copy(hi, raw).then_inc(f.w_hi, 1)

                def split_x(b):
                    for r in range(BT):
                        act.wait_ge(f.t_done, b * BT + r + 1)
                        copy(x_hi[:, :, r * P:(r + 1) * P], bank_t[r % 2][:, :].rearrange("p (k t) -> p k t", k=KC)
                             ).then_inc(f.x_hi, 1)

                def gates(b):
                    for j in range(chunks):
                        act.wait_ge(f.h_full, b * chunks + j + 1)
                        nc.scalar.activation(g_sb[:, (j % 2) * BN:(j % 2 + 1) * BN], bank_h[2 * (j % 2)][:, :], ACT.Silu
                                             ).then_inc(f.g_ready, 1)

                split_x(0)
                with act.Fori(1, BLOCKS) as b1:
                    gates(b1 - 1)
                    split_x(b1)
                gates(BLOCKS - 1)

            shared_pass(0)

            def split_w(i, u, part):
                pieces = list(expert_pieces(u))
                for k in part:
                    raw, hi, _ = pieces[k]
                    copy(hi, raw).then_inc(ex.w_hi, 1)

            def w_waits(i, u, loads):
                act.wait_ge(ex.raw_loaded[u], 48 * loads)
                at_least(act, ex.o_full, 2 * (i - 1))

            def expert_step(i, u, it, last):
                if not last:
                    w_waits(i + 1, 1 - u, it + 1 + u)
                for j, (_, fn) in enumerate(FCH):
                    if not last:
                        split_w(i + 1, 1 - u, ((0, 1), (2, 3), (4, 5))[j])
                    act.wait_ge(ex.h_full, 3 * i + j + 1)
                    nc.scalar.activation(g_sb[0:fn, j * TS:(j + 1) * TS], bank_h[j][0:fn, 0:TS], ACT.Silu).then_inc(ex.g_ready, 1)
                if not last:
                    expert_split_x(i + 1)
                    split_w(i + 1, 1 - u, (6,))
                for r in range(2):
                    act.wait_ge(ex.o_full, 2 * i + r + 1)
                    if it is not 0:
                        act.wait_ge(y_stored[u], 16 * it)
                    copy(res[:, 2 * u + r, :], bank_o[r][:, :]).then_inc(ex.o_kept, 1)

            def expert_split_x(i):
                for r in range(2):
                    act.wait_ge(ex.t_done, 2 * i + r + 1)
                    copy(x_hi[:, :, r * P:(r + 1) * P], bank_t[r][:, :].rearrange("p (k t) -> p k t", k=KC)
                         ).then_inc(ex.x_hi, 1)

            act.wait_ge(shared[0].o_full, TILES)
            act.wait_ge(res_stored[0], 16 * BLOCKS)
            w_waits(0, 0, 1)
            split_w(0, 0, range(PIECES))
            expert_split_x(0)
            for u in range(2):
                expert_step(u, u, 0, False)
            with act.Fori(1, (XT - 1) // 2) as it:
                for u in range(2):
                    expert_step(2 * it + u, u, it, False)
            expert_step(XT - 1, 0, (XT - 1) // 2, True)

            shared_pass(1)

        @block.vector
        def _(dve):
            steps = [0]

            def link(ins):
                steps[0] += 1
                ins.then_inc(dve_step, 1)
                dve.wait_ge(dve_step, steps[0])

            dve.wait_ge(consts_in, 48)
            nc.vector.memset(ones_bf[:, :], 1.0)
            nc.vector.tensor_copy(before_bf[:, :], const("before"))
            nc.vector.tensor_copy(col_bf[:, :], const("col"))
            link(nc.vector.tensor_copy(ctile_bf[:, :], const("choice_tile")))

            def front_xt(t, u):
                dve.wait_ge(ft_done, t + 1)
                at_least(dve, routed, t - 1)
                nc.vector.tensor_copy(xt[:, u % 2, :, :], bank_t[u % 2][:, :].rearrange("p (k t) -> p k t", k=KC)
                                      ).then_inc(fxt_ready, 1)

            def front_logits(t, u):
                dve.wait_ge(routed, t + 1)
                nc.vector.tensor_copy(logits[:, :, bass.ds(t, 1)].rearrange("p e t -> p (e t)"), bank_o[u % 2][:, 0:E + 1]
                                      ).then_inc(logits_kept, 1)

            for t in range(4):
                front_xt(t, t)
                if t >= 1:
                    front_logits(t - 1, t - 1)
            with dve.Fori(1, TILES // 4) as it:
                for u in range(4):
                    front_xt(4 * it + u, u)
                    front_logits(4 * it + u - 1, (u - 1) % 4)
            front_logits(TILES - 1, 3)

            def routing():
                dve.wait_ge(logits_kept, TILES)
                lg = logits[:, 0:E, :]
                rev = const("rev").rearrange("p (e t) -> p e t", e=E)

                def over_e(a):
                    return a.rearrange("p e t -> p t e")

                def spread(a):
                    return a.unsqueeze(1).to_broadcast([P, E, TILES])

                def top(values, peak, mask):
                    link(nc.vector.tensor_reduce(peak, over_e(values), AX_X, ALU.max))
                    link(nc.vector.tensor_tensor(tmp[:, :, :], values, spread(peak), ALU.is_equal))
                    link(nc.vector.tensor_tensor(tmp[:, :, :], tmp[:, :, :], rev, ALU.mult))
                    link(nc.vector.tensor_reduce(small[:, 7, :], over_e(tmp[:, :, :]), AX_X, ALU.max))
                    link(nc.vector.tensor_tensor(mask[:, :, :], rev, spread(small[:, 7, :]), ALU.is_equal))

                top(lg, small[:, 0, :], top1)
                link(nc.vector.scalar_tensor_tensor(out=rest[:, :, :], in0=top1[:, :, :], scalar=BIG, in1=lg,
                                                    op0=ALU.mult, op1=ALU.add))
                top(rest[:, :, :], small[:, 1, :], top2)
                nc.vector.tensor_tensor(both_bf[:, :, :], top1[:, :, :], top2[:, :, :], ALU.add).then_inc(both_ready, 1)
                nc.vector.tensor_tensor(small[:, 2, :], small[:, 1, :], small[:, 0, :], ALU.subtract)
                nc.vector.tensor_tensor(tmp[:, :, :], lg, spread(small[:, 0, :]), ALU.subtract).then_inc(shifted, 1)
                dve.wait_ge(exps, 2)
                link(nc.vector.tensor_reduce(small[:, 3, :], over_e(tmp[:, :, :]), AX_X, ALU.add))
                link(nc.vector.reciprocal(p_top[:, 0, :], small[:, 3, :]))
                link(nc.vector.tensor_tensor(p_top[:, 1, :], p_top[:, 0, :], small[:, 2, :], ALU.mult))
                dve.wait_ge(ranks_done, 1)
                flat = lambda a: a[:, :, :].rearrange("p e t -> p (e t)")
                link(nc.vector.tensor_copy(flat(total), bank_o[1][:, 0:E * TILES]))
                link(nc.vector.memset(tmp[:, :, :], 0.0))
                link(nc.vector.memset(percnt[:, :, :], 0.0))
                link(nc.vector.tensor_tensor_scan(out=flat(scan), data0=flat(total), data1=flat(tmp), initial=0.0,
                                                  op0=ALU.add, op1=ALU.add))
                ends = scan[:, :, TILES - 1:TILES].rearrange("p e t -> p (e t)")
                prev, cnt, tiles, upto, first, off, zero = (percnt[:, k, :] for k in range(7))
                link(nc.vector.tensor_copy(prev[:, 1:E], ends[:, 0:E - 1]))
                link(nc.vector.tensor_tensor(cnt, ends, prev, ALU.subtract))
                link(nc.vector.tensor_tensor(cmp_thr[:, :, :], cnt.unsqueeze(2).to_broadcast([P, E, THR]),
                                             const("thr").unsqueeze(1).to_broadcast([P, E, THR]), ALU.is_gt))
                link(nc.vector.tensor_reduce(tiles, cmp_thr[:, :, :], AX_X, ALU.add))
                link(nc.vector.tensor_tensor_scan(out=upto, data0=tiles, data1=zero, initial=0.0,
                                                  op0=ALU.add, op1=ALU.add))
                link(nc.vector.tensor_tensor(first, upto, tiles, ALU.subtract))
                link(nc.vector.scalar_tensor_tensor(out=off, in0=first, scalar=float(TS), in1=prev,
                                                    op0=ALU.mult, op1=ALU.subtract))
                link(nc.vector.tensor_tensor(cmp_tile[:, :, :], const("xtile", 1).unsqueeze(2).to_broadcast([1, XT, E - 1]),
                                             first[0:1, 1:E].unsqueeze(1).to_broadcast([1, XT, E - 1]), ALU.is_ge))
                link(nc.vector.tensor_reduce(te_f[:, :], cmp_tile[:, :, :], AX_X, ALU.add))
                link(nc.vector.tensor_copy(tile_expert[:, :], te_f[:, :]))
                link(nc.vector.tensor_tensor(scan[:, :, :], scan[:, :, :], total[:, :, :], ALU.subtract))
                link(nc.vector.tensor_tensor(flat(total), bank_o[0][:, 0:E * TILES], flat(scan), ALU.add))
                link(nc.vector.tensor_tensor(total[:, :, :], total[:, :, :], off.unsqueeze(2).to_broadcast([P, E, TILES]), ALU.add))
                for k, mask in enumerate((top1, top2)):
                    link(nc.vector.tensor_tensor(tmp[:, :, :], mask[:, :, :], total[:, :, :], ALU.mult))
                    link(nc.vector.tensor_reduce(posf[:, k * TILES:(k + 1) * TILES], over_e(tmp[:, :, :]), AX_X, ALU.add))
                slots = slot_of[:, :, :].rearrange("p k t -> p (k t)")
                link(nc.vector.tensor_copy(slots, posf[:, :]))
                nc.vector.tensor_scalar(hi_i[:, :], slots, 7, None, ALU.logical_shift_right)
                link(nc.vector.tensor_scalar(lo_i[:, :], slots, P - 1, None, ALU.bitwise_and))
                link(nc.vector.tensor_copy(half_bf[:, :], hi_i[:, :]))
                link(nc.vector.tensor_copy(lane_bf[:, :], lo_i[:, :]))
                for g in range(CHOICES // GRP):
                    at_least(dve, ids_used, g)
                    c = slice(g * GRP, (g + 1) * GRP)
                    nc.vector.tensor_tensor(is_lane, col_bf[:, :].unsqueeze(1).to_broadcast([P, GRP, P]),
                                            lane_bf[:, c].unsqueeze(2).to_broadcast([P, GRP, P]), ALU.is_equal)
                    link(nc.vector.tensor_tensor(is_half, col_bf[:, 0:HALVES].unsqueeze(1).to_broadcast([P, GRP, HALVES]),
                                                 half_bf[:, c].unsqueeze(2).to_broadcast([P, GRP, HALVES]), ALU.is_equal))
                    nc.vector.tensor_scalar(ids_bf[:, :, 0, :], is_half, const("pidx"), None, ALU.mult)
                    nc.vector.tensor_tensor(ids_bf[:, :, 1, :], is_half,
                                            ctile_bf[:, c].unsqueeze(2).to_broadcast([P, GRP, HALVES]), ALU.mult
                                            ).then_inc(ids_ready, 1)
                dve.wait_ge(ids_used, CHOICES // GRP)
                link(nc.vector.tensor_copy(tok_f[:, :], bank_t[0][:, 0:HALVES]))
                link(nc.vector.scalar_tensor_tensor(out=tok_f[:, :], in0=bank_t[0][:, HALVES:2 * HALVES], scalar=float(P),
                                                    in1=tok_f[:, :], op0=ALU.mult, op1=ALU.add))
                nc.vector.tensor_copy(token_of[:, :], tok_f[:, :]).then_inc(routing_done, 1)

            routing()

            def hidden(f, n, j, fn, width, bank2, tok):
                g = slice(tok * width, (tok + 1) * width)
                dve.wait_ge(f.g_ready, n + 1)
                nc.vector.tensor_tensor(h_sb[0:fn, g], bank2, g_sb[0:fn, g], ALU.mult).then_inc(f.h_mul, 1)
                dve.wait_ge(f.h_mul, n + 1)
                nc.vector.tensor_copy(h_hi[0:fn, j, 0:width], h_sb[0:fn, g]).then_inc(f.h_hi, 1)
                dve.wait_ge(f.h_hi, n + 1)
                nc.vector.tensor_tensor(h_lo[0:fn, j, 0:width], h_sb[0:fn, g], h_hi[0:fn, j, 0:width], ALU.subtract
                                        ).then_inc(f.h_lo, 1)

            def rest_x(f, n, r):
                dve.wait_ge(f.x_hi, n + 1)
                c = slice(r * P, (r + 1) * P)
                nc.vector.tensor_tensor(x_lo[:, :, c], bank_t[r % 2][:, :].rearrange("p (k t) -> p k t", k=KC),
                                        x_hi[:, :, c], ALU.subtract).then_inc(f.x_lo, 1)

            def shared_pass(n):
                f, chunks = shared[n], len(PARTS[n])
                for k, (raw, hi, lo) in enumerate(shared_pieces(n)):
                    dve.wait_ge(f.w_hi, k + 1)
                    nc.vector.tensor_tensor(lo, raw, hi, ALU.subtract).then_inc(f.w_lo, 1)

                def split_x(b):
                    for r in range(BT):
                        rest_x(f, b * BT + r, r)

                def hiddens(b):
                    for j in range(chunks):
                        hidden(f, b * chunks + j, j, P, BN, bank_h[2 * (j % 2) + 1][:, :], j % 2)

                def sums(b):
                    dve.wait_ge(res_loaded[n], 16 * (b + 1))
                    for r in range(BT):
                        t = b * BT + r
                        dve.wait_ge(f.o_full, t + 1)
                        nc.vector.scalar_tensor_tensor(out=res[:, r, :], in0=bank_o[r % 2][:, :], scalar=s_gate[:, bass.ds(t, 1)],
                                                       in1=res[:, r, :], op0=ALU.mult, op1=ALU.add).then_inc(f.o_kept, 1)
                        if n == 0:
                            continue
                        dve.wait_ge(f.o_kept, t + 1)
                        dve.wait_ge(picked_in[r % 2], 32 * (b * 2 + r // 2 + 1))
                        for k in range(2):
                            last = nc.vector.scalar_tensor_tensor(out=res[:, r, :], in0=picked[:, r % 2, k, :],
                                                                  scalar=p_top[:, k, bass.ds(t, 1)],
                                                                  in1=res[:, r, :], op0=ALU.mult, op1=ALU.add)
                            if k == 0:
                                last.then_inc(pick_half, 1)
                                dve.wait_ge(pick_half, t + 1)
                        last.then_inc(picked_used, 1)

                split_x(0)
                with dve.Fori(1, BLOCKS) as b1:
                    hiddens(b1 - 1)
                    split_x(b1)
                    sums(b1 - 1)
                hiddens(BLOCKS - 1)
                sums(BLOCKS - 1)

            dve.wait_ge(gate_ready, 1)
            shared_pass(0)

            def split_w(i, u, part):
                pieces = list(expert_pieces(u))
                for k in part:
                    raw, hi, lo = pieces[k]
                    dve.wait_ge(ex.w_hi, PIECES * i + k + 1)
                    nc.vector.tensor_tensor(lo, raw, hi, ALU.subtract).then_inc(ex.w_lo, 1)

            def expert_step(i, u, last):
                for j, (_, fn) in enumerate(FCH):
                    if not last:
                        split_w(i + 1, 1 - u, ((0, 1), (2, 3), (4, 5))[j])
                    hidden(ex, 3 * i + j, j, fn, TS, bank_h[j][0:fn, TS:2 * TS], j)
                if not last:
                    for r in range(2):
                        rest_x(ex, 2 * (i + 1) + r, r)
                    split_w(i + 1, 1 - u, (6,))

            split_w(0, 0, range(PIECES))
            for r in range(2):
                rest_x(ex, r, r)
            with dve.Fori(0, (XT - 1) // 2) as it:
                for u in range(2):
                    expert_step(2 * it + u, u, False)
            expert_step(XT - 1, 0, True)

            shared_pass(1)


def constants():
    import numpy as np
    c = {
        "ident": np.eye(P),
        "before": np.triu(np.ones((P, P)), 1),
        "rev": np.tile(np.repeat(E - np.arange(E), TILES), (P, 1)),
        "col": np.tile(np.arange(P), (P, 1)),
        "pidx": np.arange(P)[:, None],
        "choice_tile": np.tile(np.arange(CHOICES) % TILES, (P, 1)),
        "thr": np.tile(np.arange(THR) * TS, (P, 1)),
        "xtile": np.tile(np.arange(XT), (P, 1)),
    }
    return np.ascontiguousarray(np.concatenate([c[k] for k in CONST], axis=1).astype(np.float32))


def kernel(x, itok_B_0_7, L0_cond_weights, L0_ffn_gate_w, L0_ffn_expert_fc1, L0_ffn_expert_fc2, L0_ffn_expert_proj,
           L0_ffn_shared_fc1, L0_ffn_shared_fc2, L0_ffn_shared_proj, L0_ffn_shared_gate_w):
    import numpy as np
    import concourse.bacc as bacc
    from concourse import mybir as mb
    from concourse.bass_utils import run_bass_kernel_spmd

    gates = np.concatenate([np.asarray(L0_ffn_gate_w), np.asarray(L0_ffn_shared_gate_w)], axis=0)
    up = np.concatenate([np.asarray(L0_ffn_expert_fc1), np.asarray(L0_ffn_expert_fc2)], axis=1)
    sup = np.stack([np.asarray(L0_ffn_shared_fc1).reshape(SCH, P, C), np.asarray(L0_ffn_shared_fc2).reshape(SCH, P, C)], 1)
    arrays = {
        "x": np.asarray(x),
        "subj": np.asarray(itok_B_0_7).reshape(1, BATCH),
        "cond_w": np.asarray(L0_cond_weights),
        "gates": gates.T.reshape(KC, P, E + 1).transpose(1, 0, 2),
        "ew12": up.transpose(0, 2, 1).reshape(E, KC, P, 2 * F).transpose(0, 2, 1, 3).reshape(E, P, KC * 2 * F),
        "ewp": np.asarray(L0_ffn_expert_proj).transpose(0, 2, 1),
        "sw12": sup.transpose(0, 3, 1, 2).reshape(SCH, KC, P, 2 * P).transpose(0, 2, 1, 3).reshape(SCH, P, KC * 2 * P),
        "swp": np.asarray(L0_ffn_shared_proj).T.reshape(SCH, P, C),
        "consts": constants(),
    }
    nc = bacc.Bacc("TRN2", target_bir_lowering=False, num_devices=1)
    aps, sent = [], {}
    for name, a in arrays.items():
        a = np.ascontiguousarray(a)
        sent[name] = a
        aps.append(nc.dram_tensor(name, a.shape, mb.dt.from_np(a.dtype), kind="ExternalInput").ap())
    out = nc.dram_tensor("out", (BATCH, DOUT, C), mb.dt.float32, kind="ExternalOutput").ap()
    build_program(nc, *aps, out)
    r = run_bass_kernel_spmd(nc, [sent], core_ids=[0])
    return r.results[0]["out"]
```

```python
from contextlib import ExitStack

import concourse.bass as bass
from concourse import mybir

ALU = mybir.AluOpType
ACT = mybir.ActivationFunctionType
AX_X = mybir.AxisListType.X
F32 = mybir.dt.float32
F32R = mybir.dt.float32r
BF16 = mybir.dt.bfloat16
I32 = mybir.dt.int32
U32 = mybir.dt.uint32

P = 128
BATCH, CIN, C = 64, 64, 512
DOUT = 64
NSUB = 8
TOKENS = BATCH * DOUT
TILES = TOKENS // P
KC = C // P
E = 8
F = 352
FCH = [(0, 128), (128, 128), (256, 96)]
FS = 1408
SCH = FS // P
PARTS = [list(range(0, 5)), list(range(5, 11))]
REGION = [[0, 1, 2, 3, 4], [3, 4, 5, 0, 1, 2]]
EARLY = [2, 3]
BT = 4
BLOCKS = TILES // BT
BN = BT * P
TS = 256
XT = 2 * TOKENS // TS + E - 1
HALVES = 2 * XT
CHOICES = 2 * TILES
GRP = 16
THR = TOKENS // TS
BIG = -3.0e38

CONST = {}
_at = 0
for _name, _n in (("ident", P), ("before", P), ("rev", E * TILES), ("col", P), ("pidx", 1),
                  ("choice_tile", CHOICES), ("thr", THR), ("xtile", XT)):
    CONST[_name] = (_at, _n)
    _at += _n
NCONST = _at


def build_program(nc, x, subj, cond_w, gates, ew12, ewp, sw12, swp, consts, out):
    xf_dram = nc.dram_tensor("xf_rows", (TOKENS, C), F32, kind="Internal").ap()
    part_dram = nc.dram_tensor("partial_rows", (TOKENS, C), F32, kind="Internal").ap()
    slot_dram = nc.dram_tensor("slot_rows", (XT * TS, C), F32, kind="Internal").ap()
    x_rows = x.rearrange("b j t -> (b j) t")
    out_rows = out.rearrange("b j t -> (b j) t")

    ctx = ExitStack()
    with ctx:
        def sb(name, shape, dt):
            return ctx.enter_context(nc.sbuf_tensor(name, shape, dt))

        def sem(name):
            return ctx.enter_context(nc.semaphore(name))

        cst = sb("cst", [P, NCONST], F32)
        gate_w = sb("gate_w", [P, KC, E + 1], F32)
        subj_sb = sb("subj_sb", [1, BATCH], I32)
        before_bf = sb("before_bf", [P, P], BF16)
        ones_bf = sb("ones_bf", [P, P], BF16)
        col_bf = sb("col_bf", [P, P], BF16)
        ctile_bf = sb("ctile_bf", [P, CHOICES], BF16)
        logits = sb("logits", [P, E + 1, TILES], F32)
        s_gate = sb("s_gate", [P, TILES], F32)
        p_top = sb("p_top", [P, 2, TILES], F32)
        slot_of = sb("slot_of", [P, 2, TILES], I32)
        token_of = sb("token_of", [P, HALVES], I32)
        tile_expert = sb("tile_expert", [1, XT], I32)
        idx_stage = sb("idx_stage", [P, 4], I32)
        maps = sb("maps", [P, NSUB, DOUT], F32)
        wblk = sb("wblk", [P, 4, P], F32)
        rows = sb("rows", [P, 4, C], F32)
        res = sb("res", [P, 4, C], F32)
        x_hi = sb("x_hi", [P, KC, BN], F32R)
        x_lo = sb("x_lo", [P, KC, BN], F32R)
        w12_hi = sb("w12_hi", [P, 6144], F32R)
        w12_lo = sb("w12_lo", [P, 6144], F32R)
        wp_hi = sb("wp_hi", [P, 3072], F32R)
        wp_lo = sb("wp_lo", [P, 3072], F32R)
        h_hi = sb("h_hi", [P, 6, BN], F32R)
        h_lo = sb("h_lo", [P, 6, BN], F32R)
        raw12 = sb("raw12", [P, 5632], F32)
        rawp = sb("rawp", [P, 3072], F32)
        g_sb = sb("g_sb", [P, 1024], F32)
        h_sb = sb("h_sb", [P, 1024], F32)
        picked = sb("picked", [P, 2, 2, C], F32)
        first_rows = picked[:, :, :, :].rearrange("p a b c -> p (a b) c")
        xt = g_sb[:, :].rearrange("p (s k t) -> p s k t", s=2, k=KC)
        top1 = sb("top1", [P, E, TILES], F32)
        top2 = sb("top2", [P, E, TILES], F32)
        tmp = sb("tmp", [P, E, TILES], F32)
        rest = sb("rest", [P, E, TILES], F32)
        both_bf = sb("both_bf", [P, E, TILES], BF16)
        total = sb("total", [P, E, TILES], F32)
        scan = sb("scan", [P, E, TILES], F32)
        small = sb("small", [P, 8, TILES], F32)
        cmp_thr = sb("cmp_thr", [P, E, THR], F32)
        percnt = sb("percnt", [P, 8, E], F32)
        cmp_tile = sb("cmp_tile", [1, XT, E - 1], F32)
        te_f = sb("te_f", [1, XT], F32)
        posf = sb("posf", [P, CHOICES], F32)
        hi_i = sb("hi_i", [P, CHOICES], I32)
        lo_i = sb("lo_i", [P, CHOICES], I32)
        half_bf = sb("half_bf", [P, CHOICES], BF16)
        lane_bf = sb("lane_bf", [P, CHOICES], BF16)
        pick_bf = picked[:, :, :, :].rearrange("p a b c -> p (a b c)").bitcast(BF16)
        is_lane = pick_bf[:, 0:GRP * P].rearrange("p (g n) -> p g n", g=GRP)
        is_half = pick_bf[:, GRP * P:GRP * (P + HALVES)].rearrange("p (g n) -> p g n", g=GRP)
        ids_bf = sb("ids_bf", [P, GRP, 2, HALVES], BF16)
        tok_f = sb("tok_f", [P, HALVES], F32)

        def const(name, parts=P):
            a, n = CONST[name]
            return cst[0:parts, a:a + n]

        ident = const("ident")

        bank_t = [ctx.enter_context(nc.psum_tensor(f"bank_t{i}", [P, 512], F32)) for i in range(2)]
        bank_o = [ctx.enter_context(nc.psum_tensor(f"bank_o{i}", [P, 512], F32)) for i in range(2)]
        bank_h = [ctx.enter_context(nc.psum_tensor(f"bank_h{i}", [P, 512], F32)) for i in range(4)]

        consts_in = sem("consts_in")
        fx_loaded = [sem(f"fx_loaded{i}") for i in range(4)]
        maps_in = sem("maps_in")
        map_zeroed = sem("map_zeroed")
        map_ready = sem("map_ready")
        cond_done = sem("cond_done")
        frow_ready = sem("frow_ready")
        frow_stored = [sem(f"frow_stored{i}") for i in range(4)]
        ft_done = sem("ft_done")
        fxt_ready = sem("fxt_ready")
        routed = sem("routed")
        logits_kept = sem("logits_kept")
        dve_step = sem("dve_step")
        shifted = sem("shifted")
        exps = sem("exps")
        gate_ready = sem("gate_ready")
        both_ready = sem("both_ready")
        ranks_done = sem("ranks_done")
        ranks_kept = sem("ranks_kept")
        ids_ready = sem("ids_ready")
        ids_used = sem("ids_used")
        routing_done = sem("routing_done")

        class Ffn:

            def __init__(self, n):
                self.raw_loaded = [sem(f"{n}_raw{i}") for i in range(6)]
                self.w_hi = sem(f"{n}_w_hi")
                self.w_lo = sem(f"{n}_w_lo")
                self.rows_loaded = [sem(f"{n}_rows{i}") for i in range(2)]
                self.t_done = sem(f"{n}_t_done")
                self.x_hi = sem(f"{n}_x_hi")
                self.x_lo = sem(f"{n}_x_lo")
                self.h_full = sem(f"{n}_h_full")
                self.g_ready = sem(f"{n}_g_ready")
                self.h_mul = sem(f"{n}_h_mul")
                self.h_hi = sem(f"{n}_h_hi")
                self.h_lo = sem(f"{n}_h_lo")
                self.o_full = sem(f"{n}_o_full")
                self.o_kept = sem(f"{n}_o_kept")

        shared = [Ffn("s0"), Ffn("s1")]
        ex = Ffn("ex")
        res_loaded = [sem("res_loaded0"), sem("res_loaded1")]
        res_stored = [sem("res_stored0"), sem("res_stored1")]
        y_stored = [sem("y_stored0"), sem("y_stored1")]
        picked_in = [sem("picked_in0"), sem("picked_in1")]
        pick_half = sem("pick_half")
        picked_used = sem("picked_used")
        row_summed = [shared[0].o_kept, picked_used]

        def at_least(eng, s, value):
            if not isinstance(value, int) or value > 0:
                eng.wait_ge(s, value)

        def all_xf_stored(eng):
            for u in range(4):
                eng.wait_ge(frow_stored[u], 16 * (TILES // 4))

        def all_y_stored(eng):
            for u in range(2):
                eng.wait_ge(y_stored[u], 16 * ((XT + 1 - u) // 2))

        def shared_pieces(n, q):
            k = REGION[n][q]
            yield (raw12[:, (q % 5) * 1024:(q % 5 + 1) * 1024], w12_hi[:, k * 1024:(k + 1) * 1024],
                   w12_lo[:, k * 1024:(k + 1) * 1024])
            yield (rawp[:, q * 512:(q + 1) * 512], wp_hi[:, k * 512:(k + 1) * 512],
                   wp_lo[:, k * 512:(k + 1) * 512])

        def expert_pieces(u):
            for k in range(KC):
                a = u * 2816 + k * 2 * F
                yield raw12[:, a:a + 2 * F], w12_hi[:, a:a + 2 * F], w12_lo[:, a:a + 2 * F]
            for k, (_, n) in enumerate(FCH):
                a = u * 1536 + k * 512
                yield rawp[0:n, a:a + 512], wp_hi[0:n, a:a + 512], wp_lo[0:n, a:a + 512]

        PIECES = KC + len(FCH)

        block = ctx.enter_context(nc.Block())

        @block.sync
        def _(sp):
            def front_load(t, u):
                sp.dma_start(res[:, u, :], x_rows[bass.ds(t * P, P), :]).then_inc(fx_loaded[u], 16)

            def front_store(t, u):
                sp.wait_ge(frow_ready, t + 1)
                sp.dma_start(xf_dram[bass.ds(t * P, P), :], rows[:, u, :]).then_inc(frow_stored[u], 16)

            sp.dma_start(subj_sb[:, :], subj).then_inc(maps_in, 16)
            for k in range(2):
                sp.dma_start(maps[64 * k:64 * k + 64, :, :], cond_w.rearrange("s c d -> c s d")).then_inc(maps_in, 16)
            front_load(0, 0)
            sp.dma_start(cst[:, :], consts).then_inc(consts_in, 16)
            sp.dma_start(gate_w[:, :, :], gates).then_inc(consts_in, 16)
            for t in range(1, 4):
                front_load(t, t)
            with sp.Fori(0, TILES // 4 - 1) as it:
                for u in range(4):
                    sp.wait_ge(cond_done, 4 * it + u + 1)
                    front_load(4 * it + u + 4, u)
                    front_store(4 * it + u, u)

            def load_raw(n, q):
                f, ch = shared[n], PARTS[n][q]
                sp.dma_start(raw12[:, (q % 5) * 1024:(q % 5 + 1) * 1024], sw12[ch]).then_inc(f.raw_loaded[q], 16)
                sp.dma_start(rawp[:, q * 512:(q + 1) * 512], swp[ch]).then_inc(f.raw_loaded[q], 16)

            def load_rows(n, b, to):
                sp.dma_start(to, xf_dram[bass.ds(b * BN, BN), :].rearrange("(r p) c -> p r c", p=P)
                             ).then_inc(shared[n].rows_loaded[0], 16)

            def load_res(n, b):
                sp.dma_start(res[:, :, :], (x_rows, part_dram)[n][bass.ds(b * BN, BN), :].rearrange("(r p) c -> p r c", p=P)
                             ).then_inc(res_loaded[n], 16)

            def store_res(n, b):
                sp.wait_ge(row_summed[n], BT * (b + 1))
                sp.dma_start((part_dram, out_rows)[n][bass.ds(b * BN, BN), :].rearrange("(r p) c -> p r c", p=P),
                             res[:, :, :]).then_inc(res_stored[n], 16)

            def shared_step(n, b):
                sp.wait_ge(shared[n].t_done, BT * (b + 1))
                load_rows(n, b + 1, rows[:, :, :])
                store_res(n, b)
                sp.wait_ge(res_stored[n], 16 * (b + 1))
                load_res(n, b + 1)

            load_raw(0, 0)
            load_rows(0, 0, first_rows[:, :, :])
            for q in range(1, len(PARTS[0])):
                load_raw(0, q)
            for t in range(TILES - 4, TILES):
                front_store(t, t % 4)
            sp.wait_ge(cond_done, TILES)
            load_res(0, 0)
            all_xf_stored(sp)
            sp.wait_ge(ft_done, TILES)
            with sp.Fori(0, 3) as b:
                shared_step(0, b)

            def load_expert(i, u):
                e = sp.value_load(tile_expert[0:1, bass.ds(i, 1)], min_val=0, max_val=E - 1)
                sp.dma_start(raw12[:, u * 2816:(u + 1) * 2816], ew12[bass.ds(e, 1), :, :].rearrange("e p n -> (e p) n")
                             ).then_inc(ex.raw_loaded[u], 16)
                w = ewp[bass.ds(e, 1), :, :].rearrange("e f c -> (e f) c")
                sp.dma_start(rawp[:, u * 1536:u * 1536 + 1024].rearrange("p (k c) -> p k c", k=2),
                             w[0:256, :].rearrange("(k p) c -> p k c", p=P)).then_inc(ex.raw_loaded[u], 16)
                sp.dma_start(rawp[0:96, u * 1536 + 1024:(u + 1) * 1536], w[256:F, :]).then_inc(ex.raw_loaded[u], 16)

            sp.wait_ge(routing_done, 1)
            sp.wait_ge(shared[0].w_lo, 2 * len(PARTS[0]))
            load_expert(0, 0)
            load_expert(1, 1)
            with sp.Fori(3, BLOCKS - 1) as b:
                shared_step(0, b)
            store_res(0, BLOCKS - 1)

            def store_y(i, u):
                sp.wait_ge(ex.o_kept, 2 * (i + 1))
                sp.dma_start(slot_dram[bass.ds(i * TS, TS), :].rearrange("(r p) c -> p r c", p=P),
                             res[:, 2 * u:2 * u + 2, :]).then_inc(y_stored[u], 16)

            def expert_step(i, u):
                sp.wait_ge(ex.w_lo, PIECES * (i + 1))
                load_expert(i + 2, u)
                store_y(i, u)

            with sp.Fori(0, (XT - 3) // 2) as it:
                for u in range(2):
                    expert_step(2 * it + u, u)
            expert_step(XT - 3, 0)
            sp.wait_ge(ex.w_lo, PIECES * XT)
            for q in range(5):
                load_raw(1, q)
            sp.wait_ge(ex.t_done, 2 * XT)
            load_rows(1, 0, rows[:, :, :])
            store_y(XT - 2, 1)
            sp.wait_ge(shared[1].w_lo, 1)
            load_raw(1, 5)
            store_y(XT - 1, 0)
            sp.wait_ge(res_stored[0], 16 * BLOCKS)
            all_y_stored(sp)
            load_res(1, 0)
            with sp.Fori(0, BLOCKS - 1) as b:
                shared_step(1, b)
            store_res(1, BLOCKS - 1)
            sp.wait_ge(res_stored[1], 16 * BLOCKS)

        @block.gpsimd
        def _(pool):
            nc.gpsimd.memset(wblk[:, :, :], 0.0).then_inc(map_zeroed, 1)
            pool.wait_ge(map_zeroed, 1)
            pool.wait_ge(maps_in, 48)

            def front_maps(t, u):
                at_least(pool, cond_done, t - 3)
                for k in range(2):
                    s = pool.value_load(subj_sb[0:1, bass.ds(2 * t + k, 1)], min_val=0, max_val=NSUB - 1)
                    c = slice(64 * k, 64 * k + 64)
                    nc.gpsimd.tensor_copy(wblk[c, u, c], maps[c, bass.ds(s, 1), :].rearrange("p s d -> p (s d)")
                                          ).then_inc(map_ready, 1)

            for t in range(4):
                front_maps(t, t)
            with pool.Fori(1, TILES // 4) as it:
                for u in range(4):
                    front_maps(4 * it + u, u)

            pool.wait_ge(routing_done, 1)
            pool.wait_ge(shared[0].t_done, TILES)

            def gather_rows(i, u):
                at_least(pool, ex.t_done, 2 * i - 2)
                nc.gpsimd.tensor_copy(idx_stage[:, 2 * u:2 * u + 2], token_of[:, bass.ds(2 * i, 2)])
                pool.drain()
                for r in range(2):
                    s = 2 * u + r
                    pool.indirect_dma_start(rows[:, s, :], None, xf_dram,
                                            bass.IndirectOffsetOnAxis(idx_stage[:, s:s + 1].bitcast(U32), 0),
                                            ).then_inc(ex.rows_loaded[u], 16)

            gather_rows(0, 0)
            gather_rows(1, 1)
            with pool.Fori(1, (XT - 1) // 2) as it:
                for u in range(2):
                    gather_rows(2 * it + u, u)
            gather_rows(XT - 1, 0)

            all_y_stored(pool)

            def gather_slots(t, u):
                at_least(pool, picked_used, t - 1)
                nc.gpsimd.tensor_copy(idx_stage[:, 2 * u:2 * u + 2], slot_of[:, :, bass.ds(t, 1)].rearrange("p a b -> p (a b)"))
                pool.drain()
                for k in range(2):
                    pool.indirect_dma_start(picked[:, u, k, :], None, slot_dram,
                                            bass.IndirectOffsetOnAxis(idx_stage[:, 2 * u + k:2 * u + k + 1].bitcast(U32), 0),
                                            ).then_inc(picked_in[u], 16)

            pool.wait_ge(ex.rows_loaded[0], 32 * ((XT + 1) // 2))
            gather_slots(0, 0)
            gather_slots(1, 1)
            with pool.Fori(1, TILES // 2) as it:
                for u in range(2):
                    gather_slots(2 * it + u, u)

        @block.tensor
        def _(pe):

            def front_map(t, it, u):
                pe.wait_ge(fx_loaded[u], 16 * (it + 1))
                pe.wait_ge(map_ready, 2 * (t + 1))
                at_least(pe, frow_ready, t - 1)
                pe.matmul(bank_h[u % 2][:, :], wblk[:, u, :], res[:, u, :], start=True, stop=True).then_inc(cond_done, 1)

            def front_transpose(t, u):
                pe.wait_ge(frow_ready, t + 1)
                at_least(pe, fxt_ready, t - 1)
                for k in range(KC):
                    m = pe.transpose(bank_t[u % 2][:, k * P:(k + 1) * P], rows[:, u, k * P:(k + 1) * P], ident)
                m.then_inc(ft_done, 1)

            def front_route(t, u):
                pe.wait_ge(fxt_ready, t + 1)
                at_least(pe, logits_kept, t - 1)
                for k in range(KC):
                    m = pe.matmul(bank_o[u % 2][:, 0:E + 1], xt[:, u % 2, k, :], gate_w[:, k, :],
                                  start=(k == 0), stop=(k == KC - 1))
                m.then_inc(routed, 1)

            for t in range(4):
                front_map(t, 0, t)
                if t == 1:
                    pe.wait_ge(consts_in, 32)
                if t >= 1:
                    front_transpose(t - 1, t - 1)
                if t >= 2:
                    front_route(t - 2, t - 2)
            with pe.Fori(1, TILES // 4) as it:
                for u in range(4):
                    front_map(4 * it + u, it, u)
                    front_transpose(4 * it + u - 1, (u - 1) % 4)
                    front_route(4 * it + u - 2, (u - 2) % 4)
            front_transpose(TILES - 1, 3)
            front_route(TILES - 2, 2)

            def transpose_rows(f, n, r, source):
                at_least(pe, f.x_lo, n + r - 1)
                for k in range(KC):
                    m = pe.transpose(bank_t[r % 2][:, k * P:(k + 1) * P], source[:, k * P:(k + 1) * P], ident)
                m.then_inc(f.t_done, 1)

            pe.wait_ge(shared[0].rows_loaded[0], 16)
            pe.wait_ge(fxt_ready, TILES)
            transpose_rows(shared[0], 0, 0, first_rows[:, 0, :])
            transpose_rows(shared[0], 0, 1, first_rows[:, 1, :])
            front_route(TILES - 1, 3)
            transpose_rows(shared[0], 0, 2, first_rows[:, 2, :])
            transpose_rows(shared[0], 0, 3, first_rows[:, 3, :])

            def product(dst, stat, moving, first, last):
                (sh, sl), (mh, ml) = stat, moving
                pe.matmul(dst, sh, mh, start=first, stop=False)
                pe.matmul(dst, sh, ml, start=False, stop=False)
                return pe.matmul(dst, sl, mh, start=False, stop=last)

            def shared_stage1(n, b, between=None):
                f, chunks = shared[n], len(PARTS[n])
                pe.wait_ge(f.x_lo, BT * (b + 1))
                for j in range(chunks):
                    if isinstance(b, int) and b == 0:
                        pe.wait_ge(f.w_lo, 2 * j + 1)
                    last = max(q for q in range(-2, j) if q % chunks % 2 == j % 2)
                    at_least(pe, f.h_mul, b * chunks + last + 1)
                    for h in range(2):
                        for k in range(KC):
                            a = REGION[n][j] * 1024 + k * 256 + h * P
                            m = product(bank_h[2 * (j % 2) + h][:, :], (w12_hi[:, a:a + P], w12_lo[:, a:a + P]),
                                        (x_hi[:, k, :], x_lo[:, k, :]), k == 0, k == KC - 1)
                    m.then_inc(f.h_full, 1)
                    if between:
                        between(j)

            def shared_row(n, b, r):
                f, chunks = shared[n], len(PARTS[n])
                at_least(pe, f.o_kept, b * BT + r - 1)
                for j in range(chunks):
                    if r == 0:
                        pe.wait_ge(f.h_lo, b * chunks + j + 1)
                        if isinstance(b, int) and b == 0:
                            pe.wait_ge(f.w_lo, 2 * j + 2)
                    c = slice(r * P, (r + 1) * P)
                    w = slice(REGION[n][j] * 512, (REGION[n][j] + 1) * 512)
                    m = product(bank_o[r % 2][:, :], (h_hi[:, j, c], h_lo[:, j, c]),
                                (wp_hi[:, w], wp_lo[:, w]), j == 0, j == chunks - 1)
                m.then_inc(f.o_full, 1)

            def shared_step(n, b, between=None):
                shared_stage1(n, b, between)
                pe.wait_ge(shared[n].rows_loaded[0], 16 * (b + 2))
                for r in range(2):
                    transpose_rows(shared[n], (b + 1) * BT, r, rows[:, r, :])
                for r in range(BT):
                    shared_row(n, b, r)
                    if r < 2:
                        transpose_rows(shared[n], (b + 1) * BT, r + 2, rows[:, r + 2, :])

            def rank_products(j):
                if j != 0:
                    return
                both = both_bf[:, :, :].rearrange("p e t -> p (e t)")
                pe.wait_ge(both_ready, 1)
                pe.wait_ge(shared[0].o_kept, BT)
                pe.matmul(bank_o[0][:, 0:E * TILES], before_bf[:, :], both, start=True, stop=True)
                pe.matmul(bank_o[1][:, 0:E * TILES], ones_bf[:, :], both, start=True, stop=True).then_inc(ranks_done, 1)

            def slot_table(g):
                if g >= CHOICES // GRP:
                    return
                if g == 0:
                    pe.wait_ge(shared[0].o_kept, 2 * BT)
                pe.wait_ge(ids_ready, g + 1)
                for j in range(GRP):
                    m = pe.matmul(bank_o[0][:, 0:2 * HALVES], is_lane[:, j, :],
                                  ids_bf[:, j, :, :].rearrange("p a b -> p (a b)"),
                                  start=(g == 0 and j == 0), stop=(g == CHOICES // GRP - 1 and j == GRP - 1))
                m.then_inc(ids_used, 1)

            shared_step(0, 0)
            shared_stage1(0, 1, rank_products)
            pe.wait_ge(ranks_kept, 1)
            pe.wait_ge(shared[0].rows_loaded[0], 16 * 3)
            for r in range(2):
                transpose_rows(shared[0], 2 * BT, r, rows[:, r, :])
            for r in range(BT):
                shared_row(0, 1, r)
                if r < 2:
                    transpose_rows(shared[0], 2 * BT, r + 2, rows[:, r + 2, :])
            shared_stage1(0, 2, slot_table)
            pe.wait_ge(shared[0].rows_loaded[0], 16 * 4)
            for r in range(2):
                transpose_rows(shared[0], 3 * BT, r, rows[:, r, :])
            pe.wait_ge(routing_done, 1)
            for r in range(BT):
                shared_row(0, 2, r)
                if r < 2:
                    transpose_rows(shared[0], 3 * BT, r + 2, rows[:, r + 2, :])
            with pe.Fori(3, BLOCKS - 1) as b:
                shared_step(0, b)
            shared_stage1(0, BLOCKS - 1)
            pe.wait_ge(ex.rows_loaded[0], 32)
            for r in range(2):
                transpose_rows(ex, 0, r, rows[:, r, :])
            for r in range(BT):
                shared_row(0, BLOCKS - 1, r)

            def expert_stage1(i, u):
                pe.wait_ge(ex.x_lo, 2 * (i + 1))
                pe.wait_ge(ex.w_lo, PIECES * i + KC)
                for j, (f0, fn) in enumerate(FCH):
                    at_least(pe, ex.h_mul, 3 * (i - 1) + j + 1)
                    for h in range(2):
                        for k in range(KC):
                            a = u * 2816 + k * 2 * F + h * F + f0
                            m = product(bank_h[j][0:fn, h * TS:(h + 1) * TS], (w12_hi[:, a:a + fn], w12_lo[:, a:a + fn]),
                                        (x_hi[:, k, 0:TS], x_lo[:, k, 0:TS]), k == 0, k == KC - 1)
                    m.then_inc(ex.h_full, 1)

            def expert_stage2(i, u):
                pe.wait_ge(ex.w_lo, PIECES * (i + 1))
                if isinstance(i, int) and i == 0:
                    pe.wait_ge(shared[0].o_kept, TILES)
                at_least(pe, ex.o_kept, 2 * i)
                for ks in ((0, 1), (2,)):
                    pe.wait_ge(ex.h_lo, 3 * i + ks[-1] + 1)
                    for r in range(2):
                        c = slice(r * P, (r + 1) * P)
                        for k in ks:
                            fn = FCH[k][1]
                            w = slice(u * 1536 + k * 512, u * 1536 + (k + 1) * 512)
                            m = product(bank_o[r][:, :], (h_hi[0:fn, k, c], h_lo[0:fn, k, c]),
                                        (wp_hi[0:fn, w], wp_lo[0:fn, w]), k == 0, k == 2)
                        if ks == (2,):
                            m.then_inc(ex.o_full, 1)

            def expert_step(i, it, u):
                expert_stage1(i, u)
                pe.wait_ge(ex.rows_loaded[1 - u], 32 * (it + 1 + u))
                for r in range(2):
                    transpose_rows(ex, 2 * (i + 1), r, rows[:, 2 * (1 - u) + r, :])
                expert_stage2(i, u)

            for u in range(2):
                expert_step(u, 0, u)
            with pe.Fori(1, (XT - 1) // 2) as it:
                for u in range(2):
                    expert_step(2 * it + u, it, u)
            expert_stage1(XT - 1, 0)
            pe.wait_ge(shared[1].rows_loaded[0], 16)
            for r in range(2):
                transpose_rows(shared[1], 0, r, rows[:, r, :])
            expert_stage2(XT - 1, 0)
            for r in range(2, BT):
                transpose_rows(shared[1], 0, r, rows[:, r, :])

            pe.wait_ge(ex.o_kept, 2 * XT)
            shared_step(1, 0)
            with pe.Fori(1, BLOCKS - 1) as b:
                shared_step(1, b)
            shared_stage1(1, BLOCKS - 1)
            for r in range(BT):
                shared_row(1, BLOCKS - 1, r)

        @block.scalar
        def _(act):
            copy = lambda o, i: nc.scalar.activation(o, i, ACT.Copy)

            def front_rows(t, u, waits):
                act.wait_ge(cond_done, t + 1)
                if waits is not None:
                    act.wait_ge(frow_stored[u], 16 * waits)
                    act.wait_ge(ft_done, t - 3)
                copy(rows[:, u, :], bank_h[u % 2][:, :]).then_inc(frow_ready, 1)

            for t in range(4):
                front_rows(t, t, None)
            with act.Fori(1, TILES // 4) as it:
                for u in range(4):
                    front_rows(4 * it + u, u, it)

            def split_x(f, n, r):
                act.wait_ge(f.t_done, n + r + 1)
                copy(x_hi[:, :, r * P:(r + 1) * P], bank_t[r % 2][:, :].rearrange("p (k t) -> p k t", k=KC)
                     ).then_inc(f.x_hi, 1)

            def split_shared(n, q):
                act.wait_ge(shared[n].raw_loaded[q], 32)
                for raw, hi, _ in shared_pieces(n, q):
                    copy(hi, raw).then_inc(shared[n].w_hi, 1)

            def gates(n, b, ahead):
                f, chunks = shared[n], len(PARTS[n])
                for j in range(chunks):
                    if ahead and j + ahead < chunks:
                        split_shared(n, j + ahead)
                    act.wait_ge(f.h_full, b * chunks + j + 1)
                    nc.scalar.activation(g_sb[:, (j % 2) * BN:(j % 2 + 1) * BN], bank_h[2 * (j % 2)][:, :], ACT.Silu
                                         ).then_inc(f.g_ready, 1)

            def shared_pass(n, after_first=None):
                gates(n, 0, EARLY[n])
                if after_first:
                    after_first()
                for r in range(BT):
                    split_x(shared[n], BT, r)
                with act.Fori(1, BLOCKS - 1) as b:
                    gates(n, b, 0)
                    for r in range(BT):
                        split_x(shared[n], (b + 1) * BT, r)
                gates(n, BLOCKS - 1, 0)

            def routing_exps():
                act.wait_ge(shifted, 1)
                nc.scalar.activation(tmp[:, :, :], tmp[:, :, :], ACT.Exp).then_inc(exps, 1)
                nc.scalar.activation(small[:, 2, :], small[:, 2, :], ACT.Exp).then_inc(exps, 1)

            split_shared(0, 0)
            split_x(shared[0], 0, 0)
            split_x(shared[0], 0, 1)
            split_shared(0, 1)
            split_x(shared[0], 0, 2)
            split_x(shared[0], 0, 3)
            act.wait_ge(logits_kept, TILES)
            nc.scalar.activation(s_gate[:, :], logits[:, E, :], ACT.Sigmoid).then_inc(gate_ready, 1)
            shared_pass(0, routing_exps)

            def split_w(i, u, part):
                pieces = list(expert_pieces(u))
                for k in part:
                    raw, hi, _ = pieces[k]
                    copy(hi, raw).then_inc(ex.w_hi, 1)

            def w_waits(i, u, loads):
                act.wait_ge(ex.raw_loaded[u], 48 * loads)
                at_least(act, ex.o_full, 2 * (i - 1))

            def keep_y(i, u, it):
                for r in range(2):
                    act.wait_ge(ex.o_full, 2 * i + r + 1)
                    if not (isinstance(it, int) and it == 0):
                        act.wait_ge(y_stored[u], 16 * it)
                    copy(res[:, 2 * u + r, :], bank_o[r][:, :]).then_inc(ex.o_kept, 1)

            def expert_gate(i, j):
                fn = FCH[j][1]
                act.wait_ge(ex.h_full, 3 * i + j + 1)
                nc.scalar.activation(g_sb[0:fn, j * TS:(j + 1) * TS], bank_h[j][0:fn, 0:TS], ACT.Silu).then_inc(ex.g_ready, 1)

            def expert_step(i, u, it):
                w_waits(i + 1, 1 - u, it + 1 + u)
                for j in range(3):
                    split_w(i + 1, 1 - u, (2 * j, 2 * j + 1))
                    expert_gate(i, j)
                for r in range(2):
                    split_x(ex, 2 * (i + 1), r)
                split_w(i + 1, 1 - u, (6,))
                keep_y(i, u, it)

            for r in range(2):
                split_x(ex, 0, r)
            w_waits(0, 0, 1)
            split_w(0, 0, range(KC))
            act.wait_ge(shared[0].o_full, TILES)
            split_w(0, 0, range(KC, PIECES))
            act.wait_ge(res_stored[0], 16 * BLOCKS)
            for u in range(2):
                expert_step(u, u, 0)
            with act.Fori(1, (XT - 1) // 2) as it:
                for u in range(2):
                    expert_step(2 * it + u, u, it)
            act.wait_ge(ex.o_full, 2 * (XT - 1))
            for j in range(3):
                split_shared(1, j)
                expert_gate(XT - 1, j)
            for r in range(2):
                split_x(shared[1], 0, r)
            keep_y(XT - 1, 0, (XT - 1) // 2)
            for r in range(2, BT):
                split_x(shared[1], 0, r)

            shared_pass(1)

        @block.vector
        def _(dve):
            steps = [0]

            def link(ins):
                steps[0] += 1
                ins.then_inc(dve_step, 1)
                dve.wait_ge(dve_step, steps[0])

            dve.wait_ge(consts_in, 32)
            nc.vector.memset(ones_bf[:, :], 1.0)
            nc.vector.tensor_copy(before_bf[:, :], const("before"))
            nc.vector.tensor_copy(col_bf[:, :], const("col"))
            link(nc.vector.tensor_copy(ctile_bf[:, :], const("choice_tile")))

            def front_xt(t, u):
                dve.wait_ge(ft_done, t + 1)
                at_least(dve, routed, t - 1)
                nc.vector.tensor_copy(xt[:, u % 2, :, :], bank_t[u % 2][:, :].rearrange("p (k t) -> p k t", k=KC)
                                      ).then_inc(fxt_ready, 1)

            def front_logits(t, u):
                dve.wait_ge(routed, t + 1)
                nc.vector.tensor_copy(logits[:, :, bass.ds(t, 1)].rearrange("p e t -> p (e t)"), bank_o[u % 2][:, 0:E + 1]
                                      ).then_inc(logits_kept, 1)

            for t in range(4):
                front_xt(t, t)
                if t >= 1:
                    front_logits(t - 1, t - 1)
            with dve.Fori(1, TILES // 4) as it:
                for u in range(4):
                    front_xt(4 * it + u, u)
                    front_logits(4 * it + u - 1, (u - 1) % 4)
            lg = logits[:, 0:E, :]
            rev = const("rev").rearrange("p (e t) -> p e t", e=E)
            prev, cnt, tiles, upto, first, off, zero = (percnt[:, k, :] for k in range(7))

            def over_e(a):
                return a.rearrange("p e t -> p t e")

            def spread(a):
                return a.unsqueeze(1).to_broadcast([P, E, TILES])

            def flat(a):
                return a[:, :, :].rearrange("p e t -> p (e t)")

            def top(values, peak, mask):
                link(nc.vector.tensor_reduce(peak, over_e(values), AX_X, ALU.max))
                link(nc.vector.tensor_tensor(tmp[:, :, :], values, spread(peak), ALU.is_equal))
                link(nc.vector.tensor_tensor(tmp[:, :, :], tmp[:, :, :], rev, ALU.mult))
                link(nc.vector.tensor_reduce(small[:, 7, :], over_e(tmp[:, :, :]), AX_X, ALU.max))
                link(nc.vector.tensor_tensor(mask[:, :, :], rev, spread(small[:, 7, :]), ALU.is_equal))

            def route_first():
                top(lg, small[:, 0, :], top1)
                link(nc.vector.scalar_tensor_tensor(out=rest[:, :, :], in0=top1[:, :, :], scalar=BIG, in1=lg,
                                                    op0=ALU.mult, op1=ALU.add))

            def route_second():
                top(rest[:, :, :], small[:, 1, :], top2)
                nc.vector.tensor_tensor(both_bf[:, :, :], top1[:, :, :], top2[:, :, :], ALU.add).then_inc(both_ready, 1)
                nc.vector.tensor_tensor(small[:, 2, :], small[:, 1, :], small[:, 0, :], ALU.subtract)
                nc.vector.tensor_tensor(tmp[:, :, :], lg, spread(small[:, 0, :]), ALU.subtract).then_inc(shifted, 1)

            def route_weights():
                dve.wait_ge(exps, 2)
                link(nc.vector.tensor_reduce(small[:, 3, :], over_e(tmp[:, :, :]), AX_X, ALU.add))
                link(nc.vector.reciprocal(p_top[:, 0, :], small[:, 3, :]))
                link(nc.vector.tensor_tensor(p_top[:, 1, :], p_top[:, 0, :], small[:, 2, :], ALU.mult))
                link(nc.vector.memset(tmp[:, :, :], 0.0))
                link(nc.vector.memset(percnt[:, :, :], 0.0))

            def expert_starts():
                dve.wait_ge(ranks_done, 1)
                nc.vector.tensor_copy(flat(rest), bank_o[0][:, 0:E * TILES])
                nc.vector.tensor_copy(flat(total), bank_o[1][:, 0:E * TILES]).then_inc(ranks_kept, 1)
                dve.wait_ge(ranks_kept, 1)
                link(nc.vector.tensor_tensor_scan(out=flat(scan), data0=flat(total), data1=flat(tmp), initial=0.0,
                                                  op0=ALU.add, op1=ALU.add))
                ends = scan[:, :, TILES - 1:TILES].rearrange("p e t -> p (e t)")
                link(nc.vector.tensor_copy(prev[:, 1:E], ends[:, 0:E - 1]))
                link(nc.vector.tensor_tensor(cnt, ends, prev, ALU.subtract))
                link(nc.vector.tensor_tensor(cmp_thr[:, :, :], cnt.unsqueeze(2).to_broadcast([P, E, THR]),
                                             const("thr").unsqueeze(1).to_broadcast([P, E, THR]), ALU.is_gt))
                link(nc.vector.tensor_reduce(tiles, cmp_thr[:, :, :], AX_X, ALU.add))

            def tile_experts():
                link(nc.vector.tensor_tensor_scan(out=upto, data0=tiles, data1=zero, initial=0.0,
                                                  op0=ALU.add, op1=ALU.add))
                link(nc.vector.tensor_tensor(first, upto, tiles, ALU.subtract))
                link(nc.vector.scalar_tensor_tensor(out=off, in0=first, scalar=float(TS), in1=prev,
                                                    op0=ALU.mult, op1=ALU.subtract))
                link(nc.vector.tensor_tensor(cmp_tile[:, :, :], const("xtile", 1).unsqueeze(2).to_broadcast([1, XT, E - 1]),
                                             first[0:1, 1:E].unsqueeze(1).to_broadcast([1, XT, E - 1]), ALU.is_ge))
                link(nc.vector.tensor_reduce(te_f[:, :], cmp_tile[:, :, :], AX_X, ALU.add))
                link(nc.vector.tensor_copy(tile_expert[:, :], te_f[:, :]))

            def choice_slots():
                link(nc.vector.tensor_tensor(scan[:, :, :], scan[:, :, :], total[:, :, :], ALU.subtract))
                link(nc.vector.tensor_tensor(flat(total), flat(rest), flat(scan), ALU.add))
                link(nc.vector.tensor_tensor(total[:, :, :], total[:, :, :], off.unsqueeze(2).to_broadcast([P, E, TILES]), ALU.add))
                for k, mask in enumerate((top1, top2)):
                    link(nc.vector.tensor_tensor(tmp[:, :, :], mask[:, :, :], total[:, :, :], ALU.mult))
                    link(nc.vector.tensor_reduce(posf[:, k * TILES:(k + 1) * TILES], over_e(tmp[:, :, :]), AX_X, ALU.add))

            def slot_places():
                slots = slot_of[:, :, :].rearrange("p k t -> p (k t)")
                link(nc.vector.tensor_copy(slots, posf[:, :]))
                nc.vector.tensor_scalar(hi_i[:, :], slots, 7, None, ALU.logical_shift_right)
                link(nc.vector.tensor_scalar(lo_i[:, :], slots, P - 1, None, ALU.bitwise_and))
                nc.vector.tensor_copy(half_bf[:, :], hi_i[:, :])
                link(nc.vector.tensor_copy(lane_bf[:, :], lo_i[:, :]))

            def choice_ids(g):
                at_least(dve, ids_used, g)
                c = slice(g * GRP, (g + 1) * GRP)
                nc.vector.tensor_tensor(is_lane, col_bf[:, :].unsqueeze(1).to_broadcast([P, GRP, P]),
                                        lane_bf[:, c].unsqueeze(2).to_broadcast([P, GRP, P]), ALU.is_equal)
                link(nc.vector.tensor_tensor(is_half, col_bf[:, 0:HALVES].unsqueeze(1).to_broadcast([P, GRP, HALVES]),
                                             half_bf[:, c].unsqueeze(2).to_broadcast([P, GRP, HALVES]), ALU.is_equal))
                nc.vector.tensor_scalar(ids_bf[:, :, 0, :], is_half, const("pidx"), None, ALU.mult)
                nc.vector.tensor_tensor(ids_bf[:, :, 1, :], is_half,
                                        ctile_bf[:, c].unsqueeze(2).to_broadcast([P, GRP, HALVES]), ALU.mult
                                        ).then_inc(ids_ready, 1)

            def slot_tokens():
                dve.wait_ge(ids_used, CHOICES // GRP)
                link(nc.vector.tensor_copy(tok_f[:, :], bank_o[0][:, 0:HALVES]))
                link(nc.vector.scalar_tensor_tensor(out=tok_f[:, :], in0=bank_o[0][:, HALVES:2 * HALVES], scalar=float(P),
                                                    in1=tok_f[:, :], op0=ALU.mult, op1=ALU.add))
                nc.vector.tensor_copy(token_of[:, :], tok_f[:, :]).then_inc(routing_done, 1)

            def hidden(f, n, j, fn, width, bank2, tok):
                g = slice(tok * width, (tok + 1) * width)
                dve.wait_ge(f.g_ready, n + 1)
                nc.vector.tensor_tensor(h_sb[0:fn, g], bank2, g_sb[0:fn, g], ALU.mult).then_inc(f.h_mul, 1)
                dve.wait_ge(f.h_mul, n + 1)
                nc.vector.tensor_copy(h_hi[0:fn, j, 0:width], h_sb[0:fn, g]).then_inc(f.h_hi, 1)
                dve.wait_ge(f.h_hi, n + 1)
                nc.vector.tensor_tensor(h_lo[0:fn, j, 0:width], h_sb[0:fn, g], h_hi[0:fn, j, 0:width], ALU.subtract
                                        ).then_inc(f.h_lo, 1)

            def rest_x(f, n, r):
                dve.wait_ge(f.x_hi, n + 1)
                c = slice(r * P, (r + 1) * P)
                nc.vector.tensor_tensor(x_lo[:, :, c], bank_t[r % 2][:, :].rearrange("p (k t) -> p k t", k=KC),
                                        x_hi[:, :, c], ALU.subtract).then_inc(f.x_lo, 1)

            def split_shared(n, q):
                for k, (raw, hi, lo) in enumerate(shared_pieces(n, q)):
                    dve.wait_ge(shared[n].w_hi, 2 * q + k + 1)
                    nc.vector.tensor_tensor(lo, raw, hi, ALU.subtract).then_inc(shared[n].w_lo, 1)

            def hiddens(n, b, ahead=0, between=None):
                f, chunks = shared[n], len(PARTS[n])
                for j in range(chunks):
                    if ahead and j + ahead < chunks:
                        split_shared(n, j + ahead)
                    hidden(f, b * chunks + j, j, P, BN, bank_h[2 * (j % 2) + 1][:, :], j % 2)
                    if between:
                        between(j)

            def row_sum(n, b, r):
                f, t = shared[n], b * BT + r
                dve.wait_ge(f.o_full, t + 1)
                nc.vector.scalar_tensor_tensor(out=res[:, r, :], in0=bank_o[r % 2][:, :], scalar=s_gate[:, bass.ds(t, 1)],
                                               in1=res[:, r, :], op0=ALU.mult, op1=ALU.add).then_inc(f.o_kept, 1)
                if n == 0:
                    return
                dve.wait_ge(f.o_kept, t + 1)
                dve.wait_ge(picked_in[r % 2], 32 * (b * 2 + r // 2 + 1))
                for k in range(2):
                    last = nc.vector.scalar_tensor_tensor(out=res[:, r, :], in0=picked[:, r % 2, k, :],
                                                          scalar=p_top[:, k, bass.ds(t, 1)],
                                                          in1=res[:, r, :], op0=ALU.mult, op1=ALU.add)
                    if k == 0:
                        last.then_inc(pick_half, 1)
                        dve.wait_ge(pick_half, t + 1)
                last.then_inc(picked_used, 1)

            def shared_tail(n, b):
                for r in range(2):
                    rest_x(shared[n], (b + 1) * BT + r, r)
                dve.wait_ge(res_loaded[n], 16 * (b + 1))
                for r in range(BT):
                    row_sum(n, b, r)
                    if r < 2:
                        rest_x(shared[n], (b + 1) * BT + r + 2, r + 2)

            split_shared(0, 0)
            rest_x(shared[0], 0, 0)
            rest_x(shared[0], 1, 1)
            split_shared(0, 1)
            rest_x(shared[0], 2, 2)
            rest_x(shared[0], 3, 3)
            front_logits(TILES - 1, 3)

            hiddens(0, 0, EARLY[0], lambda j: {2: route_first, 3: route_second}.get(j, lambda: None)())
            dve.wait_ge(gate_ready, 1)
            shared_tail(0, 0)
            route_weights()
            hiddens(0, 1, 0, lambda j: {1: expert_starts, 2: tile_experts, 3: choice_slots, 4: slot_places}.get(j, lambda: None)())
            shared_tail(0, 1)
            choice_ids(0)
            hiddens(0, 2, 0, lambda j: choice_ids(j + 1) if j + 1 < CHOICES // GRP else slot_tokens() if j == 4 else None)
            shared_tail(0, 2)
            with dve.Fori(3, BLOCKS - 1) as b:
                hiddens(0, b)
                shared_tail(0, b)
            hiddens(0, BLOCKS - 1)

            def split_w(i, u, part):
                pieces = list(expert_pieces(u))
                for k in part:
                    raw, hi, lo = pieces[k]
                    dve.wait_ge(ex.w_hi, PIECES * i + k + 1)
                    nc.vector.tensor_tensor(lo, raw, hi, ALU.subtract).then_inc(ex.w_lo, 1)

            def expert_hidden(i, j):
                fn = FCH[j][1]
                hidden(ex, 3 * i + j, j, fn, TS, bank_h[j][0:fn, TS:2 * TS], j)

            def expert_step(i, u):
                for j in range(3):
                    split_w(i + 1, 1 - u, (2 * j, 2 * j + 1))
                    expert_hidden(i, j)
                for r in range(2):
                    rest_x(ex, 2 * (i + 1) + r, r)
                split_w(i + 1, 1 - u, (6,))

            for r in range(2):
                rest_x(ex, r, r)
            dve.wait_ge(res_loaded[0], 16 * BLOCKS)
            for r in range(BT):
                split_w(0, 0, (r,))
                row_sum(0, BLOCKS - 1, r)
            split_w(0, 0, range(KC, PIECES))
            with dve.Fori(0, (XT - 1) // 2) as it:
                for u in range(2):
                    expert_step(2 * it + u, u)
            for j in range(3):
                split_shared(1, j)
                expert_hidden(XT - 1, j)
            for r in range(BT):
                rest_x(shared[1], r, r)

            hiddens(1, 0, EARLY[1])
            shared_tail(1, 0)
            with dve.Fori(1, BLOCKS - 1) as b:
                hiddens(1, b)
                shared_tail(1, b)
            hiddens(1, BLOCKS - 1)
            dve.wait_ge(res_loaded[1], 16 * BLOCKS)
            for r in range(BT):
                row_sum(1, BLOCKS - 1, r)


def constants():
    import numpy as np
    c = {
        "ident": np.eye(P),
        "before": np.triu(np.ones((P, P)), 1),
        "rev": np.tile(np.repeat(E - np.arange(E), TILES), (P, 1)),
        "col": np.tile(np.arange(P), (P, 1)),
        "pidx": np.arange(P)[:, None],
        "choice_tile": np.tile(np.arange(CHOICES) % TILES, (P, 1)),
        "thr": np.tile(np.arange(THR) * TS, (P, 1)),
        "xtile": np.tile(np.arange(XT), (P, 1)),
    }
    return np.ascontiguousarray(np.concatenate([c[k] for k in CONST], axis=1).astype(np.float32))


def kernel(x, itok_B_0_7, L0_cond_weights, L0_ffn_gate_w, L0_ffn_expert_fc1, L0_ffn_expert_fc2, L0_ffn_expert_proj,
           L0_ffn_shared_fc1, L0_ffn_shared_fc2, L0_ffn_shared_proj, L0_ffn_shared_gate_w):
    import numpy as np
    import concourse.bacc as bacc
    from concourse import mybir as mb
    from concourse.bass_utils import run_bass_kernel_spmd

    gates = np.concatenate([np.asarray(L0_ffn_gate_w), np.asarray(L0_ffn_shared_gate_w)], axis=0)
    up = np.concatenate([np.asarray(L0_ffn_expert_fc1), np.asarray(L0_ffn_expert_fc2)], axis=1)
    sup = np.stack([np.asarray(L0_ffn_shared_fc1).reshape(SCH, P, C), np.asarray(L0_ffn_shared_fc2).reshape(SCH, P, C)], 1)
    arrays = {
        "x": np.asarray(x),
        "subj": np.asarray(itok_B_0_7).reshape(1, BATCH),
        "cond_w": np.asarray(L0_cond_weights),
        "gates": gates.T.reshape(KC, P, E + 1).transpose(1, 0, 2),
        "ew12": up.transpose(0, 2, 1).reshape(E, KC, P, 2 * F).transpose(0, 2, 1, 3).reshape(E, P, KC * 2 * F),
        "ewp": np.asarray(L0_ffn_expert_proj).transpose(0, 2, 1),
        "sw12": sup.transpose(0, 3, 1, 2).reshape(SCH, KC, P, 2 * P).transpose(0, 2, 1, 3).reshape(SCH, P, KC * 2 * P),
        "swp": np.asarray(L0_ffn_shared_proj).T.reshape(SCH, P, C),
        "consts": constants(),
    }
    nc = bacc.Bacc("TRN2", target_bir_lowering=False, num_devices=1)
    aps, sent = [], {}
    for name, a in arrays.items():
        a = np.ascontiguousarray(a)
        sent[name] = a
        aps.append(nc.dram_tensor(name, a.shape, mb.dt.from_np(a.dtype), kind="ExternalInput").ap())
    out = nc.dram_tensor("out", (BATCH, DOUT, C), mb.dt.float32, kind="ExternalOutput").ap()
    build_program(nc, *aps, out)
    r = run_bass_kernel_spmd(nc, [sent], core_ids=[0])
    return r.results[0]["out"]
```

```python
from contextlib import ExitStack

import concourse.bass as bass
from concourse import mybir

ALU = mybir.AluOpType
ACT = mybir.ActivationFunctionType
AX_X = mybir.AxisListType.X
F32 = mybir.dt.float32
F32R = mybir.dt.float32r
BF16 = mybir.dt.bfloat16
I32 = mybir.dt.int32
U32 = mybir.dt.uint32

P = 128
BATCH, CIN, C = 64, 64, 512
DOUT = 64
NSUB = 8
TOKENS = BATCH * DOUT
TILES = TOKENS // P
LEAD = 4
SLOTS = 8
FULL = (TILES - LEAD) // SLOTS
LAST = (TILES - LEAD) % SLOTS
KC = C // P
E = 8
F = 352
FCH = [(0, 128), (128, 128), (256, 96)]
FS = 1408
SCH = FS // P
UP = KC * 2 * P
E_UP = KC * 2 * F
E_DOWN = len(FCH) * C
SHARED_MOST = 6
PARTS = [list(range(0, 5)), list(range(5, 11))]
REGION = [[0, 1, 2, 3, 4], [3, 4, 5, 0, 1, 2]]
RAW12 = [[0, 1, 2, 3, 4], [3, 4, 0, 1, 2, 3]]
RAWP = [[0, 1, 2, 3, 4], [3, 4, 0, 1, 2, 5]]
EARLY = [2, 3]
BT = 4
BLOCKS = TILES // BT
BN = BT * P
TS = 256
HALVES = 2 * TOKENS // P + E - 1
WHOLE = 2 * TOKENS // TS
SINGLE = HALVES - 2 * WHOLE
XT = WHOLE + SINGLE
GROUPS = SINGLE - 1
TAIL = 2 + 4 * GROUPS + 2
KEYS = []
for _n in range(XT):
    _g, _c = divmod(_n - 2, 4)
    _s = max(0, min(_g + (_c > 0), SINGLE))
    if _n >= 2 and _n < TAIL and _c == 0:
        KEYS.append(2 * WHOLE + _g)
    else:
        KEYS.append(2 * (_n - _s) + 1)
assert sorted(KEYS) == sorted([2 * _q + 1 for _q in range(WHOLE)] + list(range(2 * WHOLE, HALVES)))
CHOICES = 2 * TILES
GRP = 8
THR = TOKENS // TS
BIG = -3.0e38

CONST = {}
_at = 0
for _name, _n in (("ident", P), ("before", P), ("rev", E * TILES), ("col", P), ("pidx", 1),
                  ("choice_tile", CHOICES), ("thr", THR), ("key", XT), ("single_key", XT)):
    CONST[_name] = (_at, _n)
    _at += _n
NCONST = _at


def build_program(nc, x, subj, cond_w, gates, ew12, ewp, sw12, swp, consts, out):
    xf_dram = nc.dram_tensor("xf_rows", (TOKENS, C), F32, kind="Internal").ap()
    xt_dram = nc.dram_tensor("xf_transposed", (TILES, P, C), F32, kind="Internal").ap()
    part_dram = nc.dram_tensor("partial_rows", (TOKENS, C), F32, kind="Internal").ap()
    slot_dram = nc.dram_tensor("slot_rows", (HALVES * P, C), F32, kind="Internal").ap()
    x_rows = x.rearrange("b j t -> (b j) t")
    out_rows = out.rearrange("b j t -> (b j) t")

    ctx = ExitStack()
    with ctx:
        def sb(name, shape, dt):
            return ctx.enter_context(nc.sbuf_tensor(name, shape, dt))

        def sem(name):
            return ctx.enter_context(nc.semaphore(name))

        cst = sb("cst", [P, NCONST], F32)
        gate_w = sb("gate_w", [P, KC, E + 1], F32)
        subj_sb = sb("subj_sb", [1, BATCH], I32)
        before_bf = sb("before_bf", [P, P], BF16)
        ones_bf = sb("ones_bf", [P, P], BF16)
        col_bf = sb("col_bf", [P, P], BF16)
        ctile_bf = sb("ctile_bf", [P, CHOICES], BF16)
        logits = sb("logits", [P, E + 1, TILES], F32)
        s_gate = sb("s_gate", [P, TILES], F32)
        p_top = sb("p_top", [P, 2, TILES], F32)
        slot_of = sb("slot_of", [P, 2, TILES], I32)
        token_of = sb("token_of", [P, HALVES], I32)
        tile_expert = sb("tile_expert", [1, XT], I32)
        idx_stage = sb("idx_stage", [P, 4], I32)
        maps = sb("maps", [P, NSUB, DOUT], F32)
        wblk = sb("wblk", [P, 4, P], F32)
        rows = sb("rows", [P, 4, C], F32)
        res = sb("res", [P, 4, C], F32)
        x_hi = sb("x_hi", [P, KC, BN], F32R)
        x_lo = sb("x_lo", [P, KC, BN], F32R)
        w12_hi = sb("w12_hi", [P, SHARED_MOST * UP], F32R)
        w12_lo = sb("w12_lo", [P, SHARED_MOST * UP], F32R)
        wp_hi = sb("wp_hi", [P, SHARED_MOST * C], F32R)
        wp_lo = sb("wp_lo", [P, SHARED_MOST * C], F32R)
        h_hi = sb("h_hi", [P, 6, BN], F32R)
        h_lo = sb("h_lo", [P, 6, BN], F32R)
        raw12 = sb("raw12", [P, 2 * E_UP], F32)
        used = len(PARTS[0])
        fx_hi_at = [w12_hi[:, used * UP + u * C:used * UP + (u + 1) * C] for u in range(2)]
        fx_lo_at = [w12_lo[:, used * UP + u * C:used * UP + (u + 1) * C] for u in range(2)]
        maps_hi, maps_lo = (h[:, used, :].rearrange("p (s d) -> p s d", s=NSUB) for h in (h_hi, h_lo))
        blk_hi, blk_lo = (w[:, used * C:(used + 1) * C].rearrange("p (u n) -> p u n", u=4) for w in (wp_hi, wp_lo))
        rawp = sb("rawp", [P, 2 * E_DOWN], F32)
        g_sb = sb("g_sb", [P, 2 * BN], F32)
        h_sb = sb("h_sb", [P, 2 * BN], F32)
        picked = sb("picked", [P, 2, 2, C], F32)
        x_tiles = picked[:, :, :, :].rearrange("p a b c -> p (a b) c")
        xt = sb("xt", [P, 2, KC, P], F32)
        xt_in = sb("xt_in", [P, BT, C], F32)
        free_at = [0]

        def temp(*shape, dt=F32, parts=P):
            n = 1
            for d in shape:
                n *= d
            words = n if dt != BF16 else n // 2
            a = raw12[0:parts, free_at[0]:free_at[0] + words]
            free_at[0] += words
            assert free_at[0] <= 2 * E_UP
            a = a if dt == F32 else a.bitcast(dt)
            names = "abc"[:len(shape)]
            return a if len(shape) == 1 else a.rearrange(
                f"p ({' '.join(names)}) -> p {' '.join(names)}", **dict(zip(names, shape)))

        top1, top2, tmp, rest, total, scan = (temp(E, TILES) for _ in range(6))
        both_bf = temp(E, TILES, dt=BF16)
        small = temp(8, TILES)
        cmp_thr = temp(E, THR)
        percnt = temp(15, E)
        cmp_tile = temp(XT, E - 1, parts=1)
        te_f = temp(XT, parts=1)
        single_f = temp(XT, parts=1)
        posf = temp(CHOICES)
        hi_i = temp(CHOICES, dt=I32)
        lo_i = temp(CHOICES, dt=I32)
        half_bf = temp(CHOICES, dt=BF16)
        lane_bf = temp(CHOICES, dt=BF16)
        ids_bf = [temp(GRP, 2, HALVES, dt=BF16) for _ in range(2)]
        tok_f = temp(HALVES)
        pick_bf = picked[:, :, :, :].rearrange("p a b c -> p (a b c)").bitcast(BF16)
        is_lane = pick_bf[:, 0:2 * GRP * P].rearrange("p (u g n) -> p u g n", u=2, g=GRP)
        is_half = pick_bf[:, 2 * GRP * P:GRP * (2 * P + HALVES)].rearrange("p (g n) -> p g n", g=GRP)

        def const(name, parts=P):
            a, n = CONST[name]
            return cst[0:parts, a:a + n]

        ident = const("ident")

        bank_t = [ctx.enter_context(nc.psum_tensor(f"bank_t{i}", [P, 512], F32)) for i in range(2)]
        bank_o = [ctx.enter_context(nc.psum_tensor(f"bank_o{i}", [P, 512], F32)) for i in range(2)]
        bank_h = [ctx.enter_context(nc.psum_tensor(f"bank_h{i}", [P, 512], F32)) for i in range(4)]

        lead_bank = bank_t + bank_o

        consts_in = sem("consts_in")
        ident_in = sem("ident_in")
        gate_w_in = sem("gate_w_in")
        fx_loaded = [sem(f"fx_loaded{i}") for i in range(4)]
        maps_in = sem("maps_in")
        map_zeroed = sem("map_zeroed")
        lead_hi = sem("lead_hi")
        lead_lo = sem("lead_lo")
        first_w_hi = sem("first_w_hi")
        map_ready = sem("map_ready")
        maps_split = sem("maps_split")
        blk_ready = sem("blk_ready")
        fx_hi = sem("fx_hi")
        fx_lo = sem("fx_lo")
        cond_done = sem("cond_done")
        frow_ready = sem("frow_ready")
        frow_stored = [sem(f"frow_stored{i}") for i in range(4)]
        ft_done = sem("ft_done")
        fxt_stored = [sem(f"fxt_stored{i}") for i in range(2)]
        fxt_ready = sem("fxt_ready")
        routed = sem("routed")
        logits_kept = sem("logits_kept")
        dve_step = sem("dve_step")
        shifted = sem("shifted")
        exps = sem("exps")
        gate_ready = sem("gate_ready")
        both_ready = sem("both_ready")
        ranks_done = sem("ranks_done")
        ranks_kept = sem("ranks_kept")
        ids_ready = sem("ids_ready")
        ids_used = sem("ids_used")
        routing_done = sem("routing_done")

        def x_count(n, b):
            return b + (0, KC)[n]

        def xt_chunk(k):
            return xt_in[:, :, k * P:(k + 1) * P]

        def chunk(x, k):
            return x[:, k, :].rearrange("p (r t) -> p r t", r=BT)

        class Ffn:

            def __init__(self, n):
                self.raw_loaded = [sem(f"{n}_raw{i}") for i in range(6)]
                self.w_hi = sem(f"{n}_w_hi")
                self.w_lo = sem(f"{n}_w_lo")
                self.rows_loaded = [sem(f"{n}_rows{i}") for i in range(1 if n in ("s0", "s1") else 2)]
                self.x_hi = sem(f"{n}_x_hi")
                self.x_lo = sem(f"{n}_x_lo")
                self.h_full = sem(f"{n}_h_full")
                self.g_ready = sem(f"{n}_g_ready")
                self.h_mul = sem(f"{n}_h_mul")
                self.h_hi = sem(f"{n}_h_hi")
                self.h_lo = sem(f"{n}_h_lo")
                self.o_full = sem(f"{n}_o_full")
                self.o_kept = sem(f"{n}_o_kept")

        shared = [Ffn("s0"), Ffn("s1")]
        ex = Ffn("ex")
        ex.t_done = sem("ex_t_done")
        single_turned = sem("single_turned")
        res_loaded = [sem("res_loaded0"), sem("res_loaded1")]
        res_stored = [sem("res_stored0"), sem("res_stored1")]
        y_stored = [sem("y_stored0"), sem("y_stored1")]
        picked_in = [sem("picked_in0"), sem("picked_in1")]
        pick_half = sem("pick_half")
        picked_used = sem("picked_used")

        def at_least(eng, s, value):
            if not isinstance(value, int) or value > 0:
                eng.wait_ge(s, value)

        def all_xf_stored(eng):
            for u in range(4):
                eng.wait_ge(frow_stored[u], 16 * (TILES // 4))

        def all_y_stored(eng):
            for u in range(2):
                eng.wait_ge(y_stored[u], 16 * ((XT + 1 - u) // 2))

        def shared_pieces(n, q):
            k = REGION[n][q]
            yield (raw12[:, RAW12[n][q] * UP:(RAW12[n][q] + 1) * UP], w12_hi[:, k * UP:(k + 1) * UP],
                   w12_lo[:, k * UP:(k + 1) * UP])
            yield (rawp[:, RAWP[n][q] * C:(RAWP[n][q] + 1) * C], wp_hi[:, k * C:(k + 1) * C],
                   wp_lo[:, k * C:(k + 1) * C])

        def expert_pieces(u):
            for k in range(KC):
                a = u * E_UP + k * 2 * F
                yield raw12[:, a:a + 2 * F], w12_hi[:, a:a + 2 * F], w12_lo[:, a:a + 2 * F]
            for k, (_, n) in enumerate(FCH):
                a = u * E_DOWN + k * C
                yield rawp[0:n, a:a + 512], wp_hi[0:n, a:a + 512], wp_lo[0:n, a:a + 512]

        PIECES = KC + len(FCH)

        block = ctx.enter_context(nc.Block())

        @block.sync
        def _(sp):
            def front_load(t, u):
                sp.dma_start(x_tiles[:, u, :], x_rows[bass.ds(t * P, P), :]).then_inc(fx_loaded[u], 16)

            def front_store(t, u):
                sp.wait_ge(frow_ready, t + 1)
                sp.dma_start(xf_dram[bass.ds(t * P, P), :], rows[:, u, :]).then_inc(frow_stored[u], 16)

            def front_store_xt(t, u):
                sp.wait_ge(fxt_ready, t + 1)
                sp.dma_start(xt_dram[bass.ds(t, 1), :, :].rearrange("t p n -> (t p) n"),
                             xt[:, u, :, :].rearrange("p k t -> p (k t)")).then_inc(fxt_stored[u], 16)

            def lead_store(t):
                front_store(t, t)
                sp.wait_ge(fxt_ready, t + 1)
                sp.dma_start(xt_dram[t], xt_in[:, t, :]).then_inc(fxt_stored[t % 2], 16)

            def front_slot(t, k, load, follows=True):
                if follows:
                    front_store_xt(t - 1, (k - 1) % 2)
                if load:
                    sp.wait_ge(cond_done, t + 1)
                    front_load(t + 4, k % 4)
                front_store(t, k % 4)

            sp.dma_start(subj_sb[:, :], subj).then_inc(maps_in, 16)
            for k in range(2):
                sp.dma_start(maps[64 * k:64 * k + 64, :, :], cond_w.rearrange("s c d -> c s d")).then_inc(maps_in, 16)
            front_load(0, 0)
            sp.dma_start(cst[:, 0:P], consts[:, 0:P]).then_inc(ident_in, 16)
            for t in range(1, 4):
                front_load(t, t)

            def load_raw(n, q):
                f, ch = shared[n], PARTS[n][q]
                up, down = RAW12[n][q], RAWP[n][q]
                sp.dma_start(raw12[:, up * UP:(up + 1) * UP], sw12[ch]).then_inc(f.raw_loaded[q], 16)
                sp.dma_start(rawp[:, down * C:(down + 1) * C], swp[ch]).then_inc(f.raw_loaded[q], 16)

            def load_xt(n, b):
                sp.dma_start(xt_in[:, :, :], xt_dram[bass.ds(b * BT, BT), :, :].rearrange("r p n -> p r n")
                             ).then_inc(shared[n].rows_loaded[0], 16)

            def load_res(n, b):
                sp.dma_start(res[:, :, :], (x_rows, part_dram)[n][bass.ds(b * BN, BN), :].rearrange("(r p) c -> p r c", p=P)
                             ).then_inc(res_loaded[n], 16)

            def store_res(n, b):
                sp.wait_ge(shared[n].o_kept, BT * (b + 1))
                sp.dma_start((part_dram, out_rows)[n][bass.ds(b * BN, BN), :].rearrange("(r p) c -> p r c", p=P),
                             res[:, :, :]).then_inc(res_stored[n], 16)

            def shared_step(n, b):
                sp.wait_ge(shared[n].x_lo, x_count(n, b))
                load_xt(n, b + 1)
                store_res(n, b)
                sp.wait_ge(res_stored[n], 16 * (b + 1))
                load_res(n, b + 1)

            def front_step(b, slots):
                first = isinstance(b, int) and b == 0
                for k in range(slots):
                    front_slot(LEAD + SLOTS * b + k, k, slots == SLOTS, not first or k > 0)
                    if k == (4 if first else 1):
                        if first:
                            sp.wait_ge(lead_lo, LEAD)
                        else:
                            sp.wait_ge(shared[0].x_lo, b)
                        if first:
                            sp.wait_ge(routed, LEAD)
                        for u in range(2):
                            sp.wait_ge(fxt_stored[u], 16 * (2 * b + 4))
                        load_xt(0, b + 1)
                if slots < SLOTS:
                    front_store_xt(TILES - 1, 1)
                store_res(0, b)
                sp.wait_ge(res_stored[0], 16 * (b + 1))
                load_res(0, b + 1)

            load_raw(0, 0)
            sp.dma_start(gate_w[:, :, :], gates).then_inc(gate_w_in, 16)
            for t in range(4):
                sp.wait_ge(cond_done, t + 1)
                front_load(t + 4, t)
                if t == 0:
                    load_raw(0, 1)
            load_raw(0, 2)
            for t in range(LEAD):
                lead_store(t)
            load_raw(0, 3)
            load_raw(0, 4)
            load_res(0, 0)
            sp.dma_start(cst[:, P:NCONST], consts[:, P:NCONST]).then_inc(consts_in, 16)
            front_step(0, SLOTS)
            with sp.Fori(1, FULL) as b:
                front_step(b, SLOTS)
            front_step(FULL, LAST)
            for u in range(2):
                sp.wait_ge(fxt_stored[u], 16 * (TILES // 2))
            with sp.Fori(FULL + 1, BLOCKS - 1) as b:
                shared_step(0, b)

            def load_expert(i, u):
                e = sp.value_load(tile_expert[0:1, bass.ds(i, 1)], min_val=0, max_val=E - 1)
                sp.dma_start(raw12[:, u * E_UP:(u + 1) * E_UP], ew12[bass.ds(e, 1), :, :].rearrange("e p n -> (e p) n")
                             ).then_inc(ex.raw_loaded[u], 16)
                w = ewp[bass.ds(e, 1), :, :].rearrange("e f c -> (e f) c")
                sp.dma_start(rawp[:, u * E_DOWN:u * E_DOWN + 2 * C].rearrange("p (k c) -> p k c", k=2),
                             w[0:2 * P, :].rearrange("(k p) c -> p k c", p=P)).then_inc(ex.raw_loaded[u], 16)
                sp.dma_start(rawp[0:FCH[2][1], u * E_DOWN + 2 * C:(u + 1) * E_DOWN], w[2 * P:F, :]).then_inc(ex.raw_loaded[u], 16)

            sp.wait_ge(routing_done, 1)
            sp.wait_ge(shared[0].w_lo, 2 * len(PARTS[0]))
            load_expert(0, 0)
            load_expert(1, 1)
            sp.wait_ge(shared[0].x_lo, BLOCKS - 1)
            load_xt(1, 0)
            store_res(0, BLOCKS - 1)

            def store_whole(i, q, u):
                sp.wait_ge(ex.o_kept, 2 * (i + 1))
                sp.dma_start(slot_dram[bass.ds(q * TS, TS), :].rearrange("(r p) c -> p r c", p=P),
                             res[:, 2 * u:2 * u + 2, :]).then_inc(y_stored[u], 16)

            def next_load(i, u):
                sp.wait_ge(ex.w_lo, PIECES * (i + 1))
                load_expert(i + 2, u)

            def whole_step(i, q, u):
                next_load(i, u)
                store_whole(i, q, u)

            def single_and_whole(i, g, q):
                next_load(i, 0)
                next_load(i + 1, 1)
                sp.wait_ge(ex.o_kept, 2 * (i + 1))
                sp.dma_start(slot_dram[bass.ds((2 * WHOLE + g) * P, P), :], res[:, 0, :]).then_inc(y_stored[0], 16)
                store_whole(i + 1, q, 1)

            for u in range(2):
                whole_step(u, u, u)
            with sp.Fori(0, GROUPS) as g:
                single_and_whole(2 + 4 * g, g, 2 + 3 * g)
                for c in range(2, 4):
                    whole_step(2 + 4 * g + c, 1 + 3 * g + c, c % 2)
            single_and_whole(TAIL - 2, GROUPS, TAIL - 1 - SINGLE)
            with sp.Fori(0, (XT - 3 - TAIL) // 2) as it:
                for u in range(2):
                    whole_step(TAIL + 2 * it + u, TAIL - SINGLE + 2 * it + u, u)
            whole_step(XT - 3, XT - 3 - SINGLE, 0)
            sp.wait_ge(ex.w_lo, PIECES * (XT - 1))
            for q in range(2):
                load_raw(1, q)
            sp.wait_ge(ex.w_lo, PIECES * XT)
            for q in range(2, 5):
                load_raw(1, q)
            store_whole(XT - 2, XT - 2 - SINGLE, 1)
            sp.wait_ge(shared[1].w_lo, 1)
            load_raw(1, 5)
            store_whole(XT - 1, XT - 1 - SINGLE, 0)
            sp.wait_ge(res_stored[0], 16 * BLOCKS)
            all_y_stored(sp)
            load_res(1, 0)
            with sp.Fori(0, BLOCKS - 1) as b:
                shared_step(1, b)
            for r in range(BT):
                t = TILES - BT + r
                sp.wait_ge(shared[1].o_kept, t + 1)
                sp.dma_start(out_rows[t * P:(t + 1) * P, :], res[:, r, :]).then_inc(res_stored[1], 16)
            sp.wait_ge(res_stored[1], 16 * (BLOCKS - 1 + BT))

        @block.gpsimd
        def _(pool):
            nc.gpsimd.memset(wblk[:, :, :], 0.0).then_inc(map_zeroed, 1)
            pool.wait_ge(map_zeroed, 1)
            pool.wait_ge(maps_in, 48)

            def front_maps(t, u):
                at_least(pool, cond_done, t - 3)
                for k in range(2):
                    s = pool.value_load(subj_sb[0:1, bass.ds(2 * t + k, 1)], min_val=0, max_val=NSUB - 1)
                    c = slice(64 * k, 64 * k + 64)
                    nc.gpsimd.tensor_copy(wblk[c, u, c], maps[c, bass.ds(s, 1), :].rearrange("p s d -> p (s d)")
                                          ).then_inc(map_ready, 1)

            for t in range(LEAD):
                front_maps(t, t)

            pool.wait_ge(map_ready, 2 * LEAD)
            nc.gpsimd.memset(wp_hi[:, used * C:(used + 1) * C].bitcast(F32), 0.0).then_inc(map_zeroed, 1)
            nc.gpsimd.memset(wp_lo[:, used * C:(used + 1) * C].bitcast(F32), 0.0).then_inc(map_zeroed, 1)
            nc.gpsimd.tensor_copy(maps_hi[:, :, :], maps[:, :, :]).then_inc(maps_split, 1)
            pool.wait_ge(maps_split, 1)
            nc.gpsimd.tensor_tensor(maps_lo[:, :, :], maps[:, :, :], maps_hi[:, :, :], ALU.subtract).then_inc(maps_split, 1)
            pool.wait_ge(maps_split, 2)
            pool.wait_ge(map_zeroed, 3)
            with pool.Fori(1, TILES // 4) as it:
                for u in range(4):
                    t = 4 * it + u
                    pool.wait_ge(cond_done, t - 3)
                    for k in range(2):
                        s = pool.value_load(subj_sb[0:1, bass.ds(2 * t + k, 1)], min_val=0, max_val=NSUB - 1)
                        c = slice(64 * k, 64 * k + 64)
                        for block, source in ((blk_hi, maps_hi), (blk_lo, maps_lo)):
                            nc.gpsimd.tensor_copy(block[c, u, c], source[c, bass.ds(s, 1), :].rearrange("p s d -> p (s d)")
                                                  ).then_inc(blk_ready, 1)

            pool.wait_ge(routing_done, 1)
            all_xf_stored(pool)

            def gather_rows(i, u, block, blocks=2):
                at_least(pool, ex.t_done, 2 * i - 2)
                nc.gpsimd.tensor_copy(idx_stage[:, 2 * u:2 * u + blocks], token_of[:, bass.ds(block, blocks)])
                pool.drain()
                for r in range(blocks):
                    s = 2 * u + r
                    pool.indirect_dma_start(rows[:, s, :], None, xf_dram,
                                            bass.IndirectOffsetOnAxis(idx_stage[:, s:s + 1].bitcast(U32), 0),
                                            ).then_inc(ex.rows_loaded[u], 16)

            for u in range(2):
                gather_rows(u, u, 2 * u)
            with pool.Fori(0, GROUPS) as g:
                gather_rows(2 + 4 * g, 0, 2 * WHOLE + g, 1)
                for c in range(1, 4):
                    gather_rows(2 + 4 * g + c, c % 2, 2 * (1 + 3 * g + c))
            gather_rows(TAIL - 2, 0, HALVES - 1, 1)
            gather_rows(TAIL - 1, 1, 2 * (TAIL - 1 - SINGLE))
            with pool.Fori(0, (XT - 1 - TAIL) // 2) as it:
                for u in range(2):
                    gather_rows(TAIL + 2 * it + u, u, 2 * (TAIL - SINGLE + u) + 4 * it)
            gather_rows(XT - 1, 0, 2 * (WHOLE - 1))

            all_y_stored(pool)

            def gather_slots(t, u):
                at_least(pool, picked_used, t - 1)
                nc.gpsimd.tensor_copy(idx_stage[:, 2 * u:2 * u + 2], slot_of[:, :, bass.ds(t, 1)].rearrange("p a b -> p (a b)"))
                pool.drain()
                for k in range(2):
                    pool.indirect_dma_start(picked[:, u, k, :], None, slot_dram,
                                            bass.IndirectOffsetOnAxis(idx_stage[:, 2 * u + k:2 * u + k + 1].bitcast(U32), 0),
                                            ).then_inc(picked_in[u], 16)

            pool.wait_ge(ex.rows_loaded[0], 32 * ((XT + 1) // 2) - 16 * SINGLE)
            gather_slots(0, 0)
            gather_slots(1, 1)
            with pool.Fori(1, TILES // 2) as it:
                for u in range(2):
                    gather_slots(2 * it + u, u)

        @block.tensor
        def _(pe):

            def front_map(t, k, bank):
                pe.wait_ge(fx_loaded[k % 4], 16)
                pe.wait_ge(map_ready, 2 * (t + 1))
                pe.matmul(bank[:, :], wblk[:, k % 4, :], x_tiles[:, k % 4, :], start=True, stop=True).then_inc(cond_done, 1)

            def front_transpose(t, k, c, bank):
                if c == 0:
                    pe.wait_ge(frow_ready, t + 1)
                    if not (isinstance(t, int) and t < LEAD):
                        pe.wait_ge(fxt_ready, t)
                m = pe.transpose(bank[:, c * P:(c + 1) * P], rows[:, k % 4, c * P:(c + 1) * P], ident)
                if c == KC - 1:
                    m.then_inc(ft_done, 1)

            def front_route(t, k, c, bank, source=None):
                if c == 0:
                    pe.wait_ge(fxt_ready, t + 1)
                    if not (isinstance(t, int) and t < 2):
                        pe.wait_ge(logits_kept, t)
                m = pe.matmul(bank[:, 0:E + 1], xt[:, k % 2, c, :] if source is None else source, gate_w[:, c, :], start=(c == 0), stop=(c == KC - 1))
                if c == KC - 1:
                    m.then_inc(routed, 1)

            for t in range(LEAD):
                front_map(t, t, bank_h[t])
            pe.wait_ge(ident_in, 16)
            for t in range(LEAD):
                for c in range(KC):
                    front_transpose(t, t, c, lead_bank[t])
            def front_piece(b, k, c, bank, slots):
                t = LEAD + SLOTS * b + k
                lead = isinstance(b, int) and b == 0
                if k <= slots and not (lead and k == 0):
                    front_transpose(t - 1, k - 1, c, bank_t[1])
                if k <= slots + 1:
                    front_route(t - 2, k - 2, c, bank, xt_in[:, t - 2, c * P:(c + 1) * P] if lead and k < 2 else None)

            def front_slot_map(b, k):
                t = LEAD + SLOTS * b + k
                pe.wait_ge(frow_ready, t)
                pe.wait_ge(blk_ready, 4 * (t - LEAD + 1))
                pe.wait_ge(fx_lo, t - LEAD + 1)
                product(bank_t[0][:, :], (blk_hi[:, k % 4, :], blk_lo[:, k % 4, :]), (fx_hi_at[k % 2], fx_lo_at[k % 2]), True, True
                        ).then_inc(cond_done, 1)

            def transpose_rows(f, n, r, source, ks=range(KC), counts=1):
                if 0 in ks:
                    at_least(pe, f.x_lo, n + r - 1)
                for k in ks:
                    m = pe.transpose(bank_t[r % 2][:, k * P:(k + 1) * P], source[:, k * P:(k + 1) * P], ident)
                if KC - 1 in ks:
                    m.then_inc(f.t_done, counts)

            def product(dst, stat, moving, first, last, small=None):
                (sh, sl), (mh, ml) = stat, moving
                for i, (a, m) in enumerate(((sh, mh), (sh, ml), (sl, mh))):
                    mm = pe.matmul(dst, a, m, start=(first and i == 0), stop=(last and i == 2))
                    if small:
                        small(i)
                return mm

            def first_chunk():
                f = shared[0]
                pe.wait_ge(frow_ready, LEAD)
                pe.wait_ge(f.w_lo, 1)
                for half in range(2):
                    pe.wait_ge(lead_lo, 2 * half + 2)
                    c = slice(half * 2 * P, (half + 1) * 2 * P)
                    for h in range(2):
                        for k in range(KC):
                            a = k * 2 * P + h * P
                            m = product(bank_h[h][:, c], (w12_hi[:, a:a + P], w12_lo[:, a:a + P]),
                                        (x_hi[:, k, c], x_lo[:, k, c]), k == 0, k == KC - 1)
                            if (half, h) == (1, 1):
                                if k == KC - 1:
                                    m.then_inc(f.h_full, 1)
                                front_piece(0, 0, k, bank_o[1], SLOTS)
                    if half == 0:
                        pe.wait_ge(gate_w_in, 16)
                        for t in range(2):
                            for k in range(KC):
                                front_route(t, t, k, bank_h[2 + t], xt_in[:, t, k * P:(k + 1) * P])
                front_slot_map(0, 0)

            def shared_stage1(n, b, between=None, front=0):
                f, chunks = shared[n], len(PARTS[n])
                first = isinstance(b, int) and b == 0
                in_pieces = first and n == 1
                if not first:
                    pe.wait_ge(f.x_lo, x_count(n, b))
                if first and n == 0:
                    first_chunk()
                for j in range(1 if first and n == 0 else 0, chunks):
                    if isinstance(b, int) and b == 0:
                        pe.wait_ge(f.w_lo, 2 * j + 1)
                    if front:
                        if j == 1:
                            pe.wait_ge(logits_kept, LEAD + SLOTS * b - 2)
                    last = max(q for q in range(-2, j) if q % chunks % 2 == j % 2)
                    at_least(pe, f.h_mul, b * chunks + last + 1)
                    for h in range(2):
                        if front and (j, h) == (0, 1):
                            at_least(pe, f.o_kept, BT * b)
                        for k in range(KC):
                            if in_pieces and (j, h) == (0, 0):
                                pe.wait_ge(f.x_lo, k + 1)
                            a = REGION[n][j] * UP + k * 2 * P + h * P
                            m = product(bank_h[2 * (j % 2) + h][:, :], (w12_hi[:, a:a + P], w12_lo[:, a:a + P]),
                                        (x_hi[:, k, :], x_lo[:, k, :]), k == 0, k == KC - 1)
                            if h == 1 and k == KC - 1:
                                m.then_inc(f.h_full, 1)
                            if h == 1 and front:
                                front_piece(b, j, k, bank_o[1], front)
                    if j < front:
                        front_slot_map(b, j)
                    if between:
                        between(j)

            def shared_row(n, b, r, front=0):
                f, chunks = shared[n], len(PARTS[n])
                at_least(pe, f.o_kept, b * BT + r - 1)
                if front and r == 1:
                    pe.wait_ge(logits_kept, LEAD + SLOTS * b + 3)
                for j in range(chunks):
                    if r == 0:
                        pe.wait_ge(f.h_lo, b * chunks + j + 1)
                        if isinstance(b, int) and b == 0:
                            pe.wait_ge(f.w_lo, 2 * j + 2)
                    c = slice(r * P, (r + 1) * P)
                    w = slice(REGION[n][j] * C, (REGION[n][j] + 1) * C)
                    m = product(bank_o[r % 2][:, :], (h_hi[:, j, c], h_lo[:, j, c]),
                                (wp_hi[:, w], wp_lo[:, w]), j == 0, j == chunks - 1)
                    if j == chunks - 1:
                        m.then_inc(f.o_full, 1)
                    if front and r < 3 and j >= 1:
                        if r == 0 and j == 1:
                            pe.wait_ge(f.h_mul, b * chunks + chunks - 1)
                        front_piece(b, chunks + r, j - 1, bank_h[3], front)
                if r < 3 and chunks + r < front:
                    front_slot_map(b, chunks + r)

            def shared_step(n, b, between=None, after_row=None, front=0):
                shared_stage1(n, b, between, front)
                for r in range(BT):
                    shared_row(n, b, r, front)
                    if after_row:
                        after_row(r)

            def rank_products():
                both = both_bf[:, :, :].rearrange("p e t -> p (e t)")
                pe.wait_ge(both_ready, 1)
                pe.matmul(bank_t[0][:, 0:E * TILES], before_bf[:, :], both, start=True, stop=True)
                pe.matmul(bank_t[1][:, 0:E * TILES], ones_bf[:, :], both, start=True, stop=True).then_inc(ranks_done, 1)

            def slot_table(g):
                pe.wait_ge(ids_ready, g + 1)
                if g == 0:
                    pe.wait_ge(ranks_kept, 1)
                for j in range(GRP):
                    m = pe.matmul(bank_t[0][:, 0:2 * HALVES], is_lane[:, g % 2, j, :],
                                  ids_bf[g % 2][:, j, :, :].rearrange("p a b -> p (a b)"),
                                  start=(g == 0 and j == 0), stop=(g == CHOICES // GRP - 1 and j == GRP - 1))
                m.then_inc(ids_used, 1)

            def at(steps):
                return lambda j: [step() for step in steps.get(j, [])]

            def table(g):
                return [lambda: slot_table(g)]

            shared_step(0, 0, front=SLOTS)
            with pe.Fori(1, FULL) as b:
                shared_step(0, b, front=SLOTS)
            shared_step(0, FULL, front=LAST)
            shared_step(0, FULL + 1, at({3: [rank_products]}))
            shared_step(0, FULL + 2, at({4: table(0)}), at({1: table(1)}))
            shared_step(0, FULL + 3, at({0: table(2), 2: table(3), 3: table(4), 4: table(5)}), at({0: table(6)}))
            shared_stage1(0, BLOCKS - 1, at({0: table(7)}))
            for r in range(BT):
                if r == 2:
                    pe.wait_ge(routing_done, 1)
                    pe.wait_ge(ex.rows_loaded[0], 32)
                    for k in range(2):
                        transpose_rows(ex, 0, k, rows[:, k, :])
                shared_row(0, BLOCKS - 1, r)

            def up_product(i, u, j, h, k, start, stop):
                f0, fn = FCH[j]
                a = u * E_UP + k * 2 * F + h * F + f0
                return product(bank_h[j][0:fn, h * TS:(h + 1) * TS], (w12_hi[:, a:a + fn], w12_lo[:, a:a + fn]),
                               (x_hi[:, k, 0:TS], x_lo[:, k, 0:TS]), start, stop)

            def whole_chunk(i, u, j):
                at_least(pe, ex.h_mul, 3 * (i - 1) + j + 1)
                for h in range(2):
                    for k in range(KC):
                        m = up_product(i, u, j, h, k, k == 0, k == KC - 1)
                m.then_inc(ex.h_full, 1)

            def expert_stage1(i, u):
                pe.wait_ge(ex.x_lo, 2 * (i + 1))
                pe.wait_ge(ex.w_lo, PIECES * i + KC)
                for j in range(3):
                    whole_chunk(i, u, j)

            def expert_stage2(i, u, row_tiles):
                pe.wait_ge(ex.w_lo, PIECES * (i + 1))
                if isinstance(i, int) and i == 0:
                    pe.wait_ge(shared[0].o_kept, TILES)
                at_least(pe, ex.o_kept, 2 * i)
                for ks in ((0, 1), (2,)):
                    pe.wait_ge(ex.h_lo, 3 * i + ks[-1] + 1)
                    for r in range(2):
                        c = slice(r * P, (r + 1) * P)
                        for k in ks:
                            fn = FCH[k][1]
                            w = slice(u * E_DOWN + k * C, u * E_DOWN + (k + 1) * C)

                            def small(pas, at=3 * (2 * r + k)):
                                q = at + pas
                                if ks != (2,) and q < row_tiles * KC:
                                    transpose_rows(ex, 2 * (i + 1), q // KC, rows[:, 2 * (1 - u) + q // KC, :], (q % KC,),
                                                   3 - row_tiles)

                            m = product(bank_o[r][:, :], (h_hi[0:fn, k, c], h_lo[0:fn, k, c]),
                                        (wp_hi[0:fn, w], wp_lo[0:fn, w]), k == 0, k == 2, small)
                        if ks == (2,):
                            m.then_inc(ex.o_full, 1)

            def whole_step(i, u, loaded, row_tiles=2):
                expert_stage1(i, u)
                pe.wait_ge(ex.rows_loaded[1 - u], loaded)
                expert_stage2(i, u, row_tiles)

            def single_up(i):
                pe.wait_ge(ex.x_lo, 2 * (i + 1))
                pe.wait_ge(ex.w_lo, PIECES * i + KC)
                for h in range(2):
                    for k in range(KC):
                        a = k * 2 * F + h * F

                        def small(pas, at=3 * k):
                            q = at + pas
                            if h == 0 and q < 2 * KC:
                                transpose_rows(ex, 2 * (i + 1), q // KC, rows[:, 2 + q // KC, :], (q % KC,))

                        m = product(bank_h[3 - h][:, 0:F], (x_hi[:, k, TS:TS + P], x_lo[:, k, TS:TS + P]),
                                    (w12_hi[:, a:a + F], w12_lo[:, a:a + F]), k == 0, k == KC - 1, small)
                    m.then_inc(ex.h_full, 1 + h)

            def single_transpose(i):
                pe.wait_ge(ex.h_mul, 3 * (i + 1))
                for j, (f0, fn) in enumerate(FCH):
                    m = pe.transpose(bank_h[3][0:fn, j * P:(j + 1) * P], h_sb[:, f0:f0 + fn], ident)
                m.then_inc(single_turned, 1)

            def single_down(i):
                pe.wait_ge(ex.w_lo, PIECES * (i + 1))
                pe.wait_ge(ex.o_kept, 2 * i)
                pe.wait_ge(ex.h_lo, 3 * (i + 1))
                for j, (_, fn) in enumerate(FCH):
                    w = slice(j * C, (j + 1) * C)
                    m = product(bank_o[0][:, :], (h_hi[0:fn, 3 + j, 0:P], h_lo[0:fn, 3 + j, 0:P]),
                                (wp_hi[0:fn, w], wp_lo[0:fn, w]), j == 0, j == 2)
                m.then_inc(ex.o_full, 2)

            def single_and_whole(i, g, loaded, loaded_next):
                pe.wait_ge(ex.rows_loaded[1], loaded)
                single_up(i)
                pe.wait_ge(ex.x_lo, 2 * (i + 2))
                for k in range(KC):
                    pe.wait_ge(ex.w_lo, PIECES * (i + 1) + k + 1)
                    for j in range(2):
                        for h in range(2):
                            m = up_product(i + 1, 1, j, h, k, k == 0 and h == 0, k == KC - 1 and h == 1)
                        if k == KC - 1:
                            m.then_inc(ex.h_full, 1)
                    if k == 0:
                        single_transpose(i)
                single_down(i)
                whole_chunk(i + 1, 1, 2)
                pe.wait_ge(ex.rows_loaded[0], loaded_next)
                expert_stage2(i + 1, 1, 2)

            whole_step(0, 0, 32)
            whole_step(1, 1, 48, 1)
            with pe.Fori(0, GROUPS) as g:
                single_and_whole(2 + 4 * g, g, 64 * g + 64, 48 * g + 80)
                whole_step(4 + 4 * g, 0, 64 * g + 96)
                whole_step(5 + 4 * g, 1, 48 * g + 96, 1)
            before = 48 * GROUPS + 48
            single_and_whole(TAIL - 2, GROUPS, 16 * TAIL, before + 32)
            with pe.Fori(0, (XT - 1 - TAIL) // 2) as it:
                whole_step(TAIL + 2 * it, 0, 32 * it + 16 * TAIL + 32)
                whole_step(TAIL + 1 + 2 * it, 1, 32 * it + before + 64)
            expert_stage1(XT - 1, 0)
            expert_stage2(XT - 1, 0, 0)

            shared_stage1(1, 0)
            pe.wait_ge(ex.o_kept, 2 * XT)
            for r in range(BT):
                shared_row(1, 0, r)
            with pe.Fori(1, BLOCKS - 1) as b:
                shared_step(1, b)
            shared_stage1(1, BLOCKS - 1)
            for r in range(BT):
                shared_row(1, BLOCKS - 1, r)

        @block.scalar
        def _(act):
            copy = lambda o, i: nc.scalar.activation(o, i, ACT.Copy)

            def front_rows(t, k, bank, stores):
                act.wait_ge(cond_done, t + 1)
                if not (isinstance(stores, int) and stores == 0):
                    act.wait_ge(frow_stored[k % 4], 16 * stores)
                    act.wait_ge(ft_done, t - 3)
                copy(rows[:, k % 4, :], bank[:, :]).then_inc(frow_ready, 1)

            def split_fx(t, k, loads):
                act.wait_ge(fx_loaded[k % 4], 16 * loads)
                copy(fx_hi_at[k % 2], x_tiles[:, k % 4, :]).then_inc(fx_hi, 1)

            def front_slot(b, k):
                front_rows(LEAD + SLOTS * b + k, k, bank_t[0], 2 * b + (LEAD + k) // 4)
                if not (isinstance(b, int) and b == FULL and k == LAST - 1):
                    split_fx(LEAD + SLOTS * b + k + 1, k + 1, 2 * b + (LEAD + k + 1) // 4 + 1)

            def split_xt(n, b):
                f = shared[n]
                act.wait_ge(f.rows_loaded[0], 16 * (b + n))
                copy(x_hi[:, :, :].rearrange("p k (r t) -> p r k t", r=BT),
                     xt_in[:, :, :].rearrange("p r (k t) -> p r k t", k=KC)).then_inc(f.x_hi, 1)

            def split_x(f, n, r):
                act.wait_ge(f.t_done, n + r + 1)
                copy(x_hi[:, :, r * P:(r + 1) * P], bank_t[r % 2][:, :].rearrange("p (k t) -> p k t", k=KC)
                     ).then_inc(f.x_hi, 1)

            def split_shared(n, q, part=(0, 1)):
                act.wait_ge(shared[n].raw_loaded[q], 32)
                pieces = list(shared_pieces(n, q))
                for k in part:
                    raw, hi, _ = pieces[k]
                    copy(hi, raw).then_inc(shared[n].w_hi, 1)

            def gates(n, b, ahead=0, front=0):
                f, chunks = shared[n], len(PARTS[n])
                for j in range(chunks):
                    if ahead and j + ahead < chunks:
                        split_shared(n, j + ahead)
                    act.wait_ge(f.h_full, b * chunks + j + 1)
                    nc.scalar.activation(g_sb[:, (j % 2) * BN:(j % 2 + 1) * BN], bank_h[2 * (j % 2)][:, :], ACT.Silu
                                         ).then_inc(f.g_ready, 1)
                    if j < front:
                        front_slot(b, j)

            def block_gate(b):
                rest = isinstance(b, int) and b == FULL + 1
                act.wait_ge(logits_kept, TILES if rest else BT * (b + 1))
                ts = slice(b * BT, TILES) if rest else bass.ds(b * BT, BT)
                nc.scalar.activation(s_gate[:, ts], logits[:, E, ts], ACT.Sigmoid).then_inc(gate_ready, 1)

            def shared_step(n, b, ahead=0, front=0, gate=True):
                gates(n, b, ahead, front)
                if n == 0 and gate:
                    block_gate(b)
                late = SLOTS - 1 if front == SLOTS else len(PARTS[0])
                for k in range(len(PARTS[0]), late):
                    front_slot(b, k)
                split_xt(n, b + 1)
                for k in range(late, front):
                    front_slot(b, k)

            def routing_exps():
                act.wait_ge(shifted, 1)
                nc.scalar.activation(tmp[:, :, :], tmp[:, :, :], ACT.Exp).then_inc(exps, 1)
                nc.scalar.activation(small[:, 2, :], small[:, 2, :], ACT.Exp).then_inc(exps, 1)

            for t in range(LEAD):
                front_rows(t, t, bank_h[t], 0)
            for t in range(LEAD):
                act.wait_ge(fxt_ready, t + 1)
                copy(x_hi[:, :, t * P:(t + 1) * P], xt_in[:, t, :].rearrange("p (k t) -> p k t", k=KC)
                     ).then_inc(lead_hi, 1)
            split_shared(0, 0, (1,))
            split_shared(0, 1)
            split_fx(LEAD, 0, 2)
            shared_step(0, 0, EARLY[0], SLOTS)
            with act.Fori(1, FULL) as b:
                shared_step(0, b, front=SLOTS)
            shared_step(0, FULL, front=LAST)
            shared_step(0, FULL + 1)
            routing_exps()
            with act.Fori(FULL + 2, BLOCKS - 1) as b:
                shared_step(0, b, gate=False)
            gates(0, BLOCKS - 1)

            def split_w(i, u, part):
                pieces = list(expert_pieces(u))
                for k in part:
                    raw, hi, _ = pieces[k]
                    copy(hi, raw).then_inc(ex.w_hi, 1)

            def w_waits(i, u, loads):
                act.wait_ge(ex.raw_loaded[u], 48 * loads)
                at_least(act, ex.o_full, 2 * (i - 1))

            def keep_y(i, u, stores):
                for r in range(2):
                    act.wait_ge(ex.o_full, 2 * i + r + 1)
                    if not (isinstance(stores, int) and stores == 0):
                        act.wait_ge(y_stored[u], 16 * stores)
                    elif r == 0:
                        act.wait_ge(res_stored[0], 16 * BLOCKS)
                    copy(res[:, 2 * u + r, :], bank_o[r][:, :]).then_inc(ex.o_kept, 1)

            def expert_gate(i, j):
                fn = FCH[j][1]
                act.wait_ge(ex.h_full, 3 * i + j + 1)
                nc.scalar.activation(g_sb[0:fn, j * TS:(j + 1) * TS], bank_h[j][0:fn, 0:TS], ACT.Silu).then_inc(ex.g_ready, 1)

            def whole_step(i, u, it, gate_first=False, row_tiles=2):
                for j in range(3):
                    if gate_first:
                        expert_gate(i, j)
                    if j == 0:
                        w_waits(i + 1, 1 - u, it + 1 + u)
                    split_w(i + 1, 1 - u, (2 * j, 2 * j + 1))
                    if not gate_first:
                        expert_gate(i, j)
                if row_tiles == 1:
                    act.wait_ge(ex.t_done, 2 * (i + 2))
                    copy(x_hi[:, :, TS:TS + P], bank_t[0][:, :].rearrange("p (k t) -> p k t", k=KC)).then_inc(ex.x_hi, 2)
                else:
                    for r in range(2):
                        split_x(ex, 2 * (i + 1), r)
                split_w(i + 1, 1 - u, (6,))
                keep_y(i, u, it)

            def single_and_whole(i, g, it):
                w_waits(i + 1, 1, it + 1)
                split_w(i + 1, 1, (0, 1))
                for r in range(2):
                    split_x(ex, 2 * (i + 1), r)
                act.wait_ge(ex.h_full, 3 * i + 1)
                nc.scalar.activation(g_sb[:, 0:F], bank_h[3][:, 0:F], ACT.Silu).then_inc(ex.g_ready, 3)
                split_w(i + 1, 1, range(2, PIECES))
                act.wait_ge(single_turned, g + 1)
                for j in (slice(0, 2), slice(2, 3)):
                    fn = FCH[j.start][1]
                    copy(h_hi[0:fn, 3 + j.start:3 + j.stop, 0:P],
                         bank_h[3][0:fn, j.start * P:j.stop * P].rearrange("p (j t) -> p j t", t=P)
                         ).then_inc(ex.h_hi, 2 - j.start // 2)
                for j in range(2):
                    expert_gate(i + 1, j)
                act.wait_ge(ex.o_full, 2 * (i + 1))
                act.wait_ge(y_stored[0], 16 * it)
                copy(res[:, 0, :], bank_o[0][:, :]).then_inc(ex.o_kept, 2)
                w_waits(i + 2, 0, it + 2)
                split_w(i + 2, 0, (0, 1))
                expert_gate(i + 1, 2)
                split_w(i + 2, 0, (2, 3))
                for r in range(2):
                    split_x(ex, 2 * (i + 2), r)
                split_w(i + 2, 0, range(KC, PIECES))
                keep_y(i + 1, 1, it)

            w_waits(0, 0, 1)
            split_w(0, 0, range(KC))
            for r in range(2):
                split_x(ex, 0, r)
            act.wait_ge(shared[0].o_full, TILES)
            split_w(0, 0, range(KC, PIECES))
            whole_step(0, 0, 0, True)
            whole_step(1, 1, 0, row_tiles=1)
            with act.Fori(0, GROUPS) as g:
                single_and_whole(2 + 4 * g, g, 2 * g + 1)
                whole_step(4 + 4 * g, 0, 2 * g + 2)
                whole_step(5 + 4 * g, 1, 2 * g + 2, row_tiles=1)
            single_and_whole(TAIL - 2, GROUPS, TAIL // 2 - 1)
            with act.Fori(TAIL // 2, (XT - 1) // 2) as it:
                for u in range(2):
                    whole_step(2 * it + u, u, it)
            act.wait_ge(ex.o_full, 2 * (XT - 1))
            for j in range(3):
                if j < 2:
                    split_shared(1, j)
                expert_gate(XT - 1, j)
            act.wait_ge(shared[1].rows_loaded[0], 16)
            for k in range(KC):
                copy(chunk(x_hi, k), xt_chunk(k)).then_inc(shared[1].x_hi, 1)
            split_shared(1, 2)
            keep_y(XT - 1, 0, (XT - 1) // 2)
            shared_step(1, 0, EARLY[1])
            with act.Fori(1, BLOCKS - 1) as b:
                shared_step(1, b)
            gates(1, BLOCKS - 1)

        @block.vector
        def _(dve):
            steps = [0]

            def link(ins):
                steps[0] += 1
                ins.then_inc(dve_step, 1)
                dve.wait_ge(dve_step, steps[0])

            def front_xt(t, k, bank, stores):
                dve.wait_ge(ft_done, t + 1)
                at_least(dve, routed, t - 1)
                if not (isinstance(stores, int) and stores == 0):
                    dve.wait_ge(fxt_stored[k % 2], 16 * stores)
                nc.vector.tensor_copy(xt[:, k % 2, :, :], bank[:, :].rearrange("p (k t) -> p k t", k=KC)
                                      ).then_inc(fxt_ready, 1)

            def front_logits(t, bank):
                dve.wait_ge(routed, t + 1)
                nc.vector.tensor_copy(logits[:, :, bass.ds(t, 1)].rearrange("p e t -> p (e t)"), bank[:, 0:E + 1]
                                      ).then_inc(logits_kept, 1)

            def front_slot(b, k, slots):
                t = LEAD + SLOTS * b + k
                if k < slots:
                    dve.wait_ge(fx_hi, t - LEAD + 1)
                    nc.vector.tensor_tensor(fx_lo_at[k % 2], x_tiles[:, k % 4, :], fx_hi_at[k % 2], ALU.subtract
                                            ).then_inc(fx_lo, 1)
                if k <= slots and not (isinstance(b, int) and b == 0 and k == 0):
                    front_xt(t - 1, k - 1, bank_t[1], 4 * b + (LEAD + k - 1) // 2)
                if k <= slots + 1:
                    front_logits(t - 2, bank_o[1] if k < len(PARTS[0]) else bank_h[3])

            lg = logits[:, 0:E, :]
            rev = const("rev").rearrange("p (e t) -> p e t", e=E)
            (prev, cnt, tiles, pairs, over, upto, first, odd, odd_upto, odd_first, limit, base, jump, shift, zero) = (
                percnt[:, k, :] for k in range(15))

            def over_e(a):
                return a.rearrange("p e t -> p t e")

            def spread(a):
                return a.unsqueeze(1).to_broadcast([P, E, TILES])

            def by_expert(a):
                return a.unsqueeze(2).to_broadcast([P, E, TILES])

            def flat(a):
                return a.rearrange("p e t -> p (e t)")

            def top(values, peak, mask):
                link(nc.vector.tensor_reduce(peak, over_e(values), AX_X, ALU.max))
                link(nc.vector.tensor_tensor(tmp[:, :, :], values, spread(peak), ALU.is_equal))
                link(nc.vector.tensor_tensor(tmp[:, :, :], tmp[:, :, :], rev, ALU.mult))
                link(nc.vector.tensor_reduce(small[:, 7, :], over_e(tmp[:, :, :]), AX_X, ALU.max))
                link(nc.vector.tensor_tensor(mask[:, :, :], rev, spread(small[:, 7, :]), ALU.is_equal))

            def route_first():
                top(lg, small[:, 0, :], top1)
                link(nc.vector.scalar_tensor_tensor(out=rest[:, :, :], in0=top1[:, :, :], scalar=BIG, in1=lg,
                                                    op0=ALU.mult, op1=ALU.add))

            def route_second():
                top(rest[:, :, :], small[:, 1, :], top2)
                nc.vector.tensor_tensor(both_bf[:, :, :], top1[:, :, :], top2[:, :, :], ALU.add).then_inc(both_ready, 1)
                nc.vector.tensor_tensor(small[:, 2, :], small[:, 1, :], small[:, 0, :], ALU.subtract)
                nc.vector.tensor_tensor(tmp[:, :, :], lg, spread(small[:, 0, :]), ALU.subtract).then_inc(shifted, 1)

            def route_weights():
                dve.wait_ge(exps, 2)
                link(nc.vector.tensor_reduce(small[:, 3, :], over_e(tmp[:, :, :]), AX_X, ALU.add))
                link(nc.vector.reciprocal(p_top[:, 0, :], small[:, 3, :]))
                link(nc.vector.tensor_tensor(p_top[:, 1, :], p_top[:, 0, :], small[:, 2, :], ALU.mult))
                link(nc.vector.memset(tmp[:, :, :], 0.0))
                link(nc.vector.memset(percnt[:, :, :], 0.0))

            def expert_starts():
                dve.wait_ge(ranks_done, 1)
                nc.vector.tensor_copy(flat(rest), bank_t[0][:, 0:E * TILES])
                nc.vector.tensor_copy(flat(total), bank_t[1][:, 0:E * TILES]).then_inc(ranks_kept, 1)
                dve.wait_ge(ranks_kept, 1)
                link(nc.vector.tensor_tensor_scan(out=flat(scan), data0=flat(total), data1=flat(tmp), initial=0.0,
                                                  op0=ALU.add, op1=ALU.add))
                ends = scan[:, :, TILES - 1:TILES].rearrange("p e t -> p (e t)")
                link(nc.vector.tensor_copy(prev[:, 1:E], ends[:, 0:E - 1]))
                link(nc.vector.tensor_tensor(cnt, ends, prev, ALU.subtract))
                link(nc.vector.tensor_tensor(cmp_thr[:, :, :], cnt.unsqueeze(2).to_broadcast([P, E, THR]),
                                             const("thr").unsqueeze(1).to_broadcast([P, E, THR]), ALU.is_gt))
                link(nc.vector.tensor_reduce(tiles, cmp_thr[:, :, :], AX_X, ALU.add))
                link(nc.vector.tensor_scalar(over, cnt, float(P), None, ALU.subtract))
                link(nc.vector.tensor_tensor(cmp_thr[:, :, :], over.unsqueeze(2).to_broadcast([P, E, THR]),
                                             const("thr").unsqueeze(1).to_broadcast([P, E, THR]), ALU.is_gt))
                link(nc.vector.tensor_reduce(pairs, cmp_thr[:, :, :], AX_X, ALU.add))

            def slot_bases():
                link(nc.vector.tensor_scalar(shift, pairs, 2.0, None, ALU.mult))
                link(nc.vector.tensor_scalar(limit, pairs, float(TS), None, ALU.mult))
                link(nc.vector.tensor_tensor_scan(out=upto, data0=shift, data1=zero, initial=0.0,
                                                  op0=ALU.add, op1=ALU.add))
                link(nc.vector.tensor_tensor(first, upto, shift, ALU.subtract))
                link(nc.vector.tensor_tensor(odd, tiles, pairs, ALU.subtract))
                link(nc.vector.tensor_tensor_scan(out=odd_upto, data0=odd, data1=zero, initial=0.0,
                                                  op0=ALU.add, op1=ALU.add))
                link(nc.vector.tensor_tensor(odd_first, odd_upto, odd, ALU.subtract))
                link(nc.vector.tensor_scalar(base, first, float(P), None, ALU.mult))
                link(nc.vector.tensor_tensor(jump, upto, odd_first, ALU.add))
                link(nc.vector.tensor_scalar(jump, jump, float(-P), float((HALVES - 1) * P), ALU.mult, ALU.add))

            def tile_experts():
                for key, starts, count in (("key", first, te_f), ("single_key", odd_first, single_f)):
                    link(nc.vector.tensor_tensor(cmp_tile[:, :, :], const(key, 1).unsqueeze(2).to_broadcast([1, XT, E - 1]),
                                                 starts[0:1, 1:E].unsqueeze(1).to_broadcast([1, XT, E - 1]), ALU.is_ge))
                    link(nc.vector.tensor_reduce(count, cmp_tile[:, :, :], AX_X, ALU.add))
                link(nc.vector.tensor_scalar(single_f, single_f, float(E - 1), None, ALU.subtract))
                link(nc.vector.tensor_tensor(cmp_tile[:, :, 0], const("key", 1), upto[0:1, E - 1:E].to_broadcast([1, XT]), ALU.is_ge))
                link(nc.vector.tensor_tensor(single_f, single_f, cmp_tile[:, :, 0], ALU.mult))
                link(nc.vector.tensor_tensor(te_f, te_f, single_f, ALU.add))
                link(nc.vector.tensor_copy(tile_expert[:, :], te_f))

            def choice_slots():
                link(nc.vector.tensor_tensor(scan[:, :, :], scan[:, :, :], total[:, :, :], ALU.subtract))
                link(nc.vector.tensor_tensor(flat(total), flat(rest), flat(scan), ALU.add))
                link(nc.vector.tensor_tensor(total, total, by_expert(prev), ALU.subtract))
                link(nc.vector.tensor_tensor(tmp, total, by_expert(limit), ALU.is_ge))
                link(nc.vector.tensor_tensor(tmp, tmp, by_expert(jump), ALU.mult))
                link(nc.vector.tensor_tensor(total, total, by_expert(base), ALU.add))
                link(nc.vector.tensor_tensor(total, total, tmp, ALU.add))
                for k, mask in enumerate((top1, top2)):
                    link(nc.vector.tensor_tensor(tmp[:, :, :], mask[:, :, :], total[:, :, :], ALU.mult))
                    link(nc.vector.tensor_reduce(posf[:, k * TILES:(k + 1) * TILES], over_e(tmp[:, :, :]), AX_X, ALU.add))

            def slot_places():
                slots = slot_of[:, :, :].rearrange("p k t -> p (k t)")
                link(nc.vector.tensor_copy(slots, posf[:, :]))
                nc.vector.tensor_scalar(hi_i[:, :], slots, 7, None, ALU.logical_shift_right)
                link(nc.vector.tensor_scalar(lo_i[:, :], slots, P - 1, None, ALU.bitwise_and))
                nc.vector.tensor_copy(half_bf[:, :], hi_i[:, :])
                link(nc.vector.tensor_copy(lane_bf[:, :], lo_i[:, :]))

            def choice_ids(g):
                at_least(dve, ids_used, g - 1)
                c = slice(g * GRP, (g + 1) * GRP)
                nc.vector.tensor_tensor(is_lane[:, g % 2, :, :], col_bf[:, :].unsqueeze(1).to_broadcast([P, GRP, P]),
                                        lane_bf[:, c].unsqueeze(2).to_broadcast([P, GRP, P]), ALU.is_equal)
                link(nc.vector.tensor_tensor(is_half, col_bf[:, 0:HALVES].unsqueeze(1).to_broadcast([P, GRP, HALVES]),
                                             half_bf[:, c].unsqueeze(2).to_broadcast([P, GRP, HALVES]), ALU.is_equal))
                nc.vector.tensor_scalar(ids_bf[g % 2][:, :, 0, :], is_half, const("pidx"), None, ALU.mult)
                nc.vector.tensor_tensor(ids_bf[g % 2][:, :, 1, :], is_half,
                                        ctile_bf[:, c].unsqueeze(2).to_broadcast([P, GRP, HALVES]), ALU.mult
                                        ).then_inc(ids_ready, 1)

            def slot_tokens():
                dve.wait_ge(ids_used, CHOICES // GRP)
                link(nc.vector.tensor_copy(tok_f[:, :], bank_t[0][:, 0:HALVES]))
                link(nc.vector.scalar_tensor_tensor(out=tok_f[:, :], in0=bank_t[0][:, HALVES:2 * HALVES], scalar=float(P),
                                                    in1=tok_f[:, :], op0=ALU.mult, op1=ALU.add))
                nc.vector.tensor_copy(token_of[:, :], tok_f[:, :]).then_inc(routing_done, 1)

            def hidden(f, n, j, fn, width, bank2, tok):
                g = slice(tok * width, (tok + 1) * width)
                dve.wait_ge(f.g_ready, n + 1)
                nc.vector.tensor_tensor(h_sb[0:fn, g], bank2, g_sb[0:fn, g], ALU.mult).then_inc(f.h_mul, 1)
                dve.wait_ge(f.h_mul, n + 1)
                nc.vector.tensor_copy(h_hi[0:fn, j, 0:width], h_sb[0:fn, g]).then_inc(f.h_hi, 1)
                dve.wait_ge(f.h_hi, n + 1)
                nc.vector.tensor_tensor(h_lo[0:fn, j, 0:width], h_sb[0:fn, g], h_hi[0:fn, j, 0:width], ALU.subtract
                                        ).then_inc(f.h_lo, 1)

            def rest_x(f, n, r):
                dve.wait_ge(f.x_hi, n + 1)
                c = slice(r * P, (r + 1) * P)
                nc.vector.tensor_tensor(x_lo[:, :, c], bank_t[r % 2][:, :].rearrange("p (k t) -> p k t", k=KC),
                                        x_hi[:, :, c], ALU.subtract).then_inc(f.x_lo, 1)

            def split_shared(n, q, part=(0, 1)):
                pieces = list(shared_pieces(n, q))
                for k in part:
                    raw, hi, lo = pieces[k]
                    dve.wait_ge(shared[n].w_hi, 2 * q + k + n)
                    nc.vector.tensor_tensor(lo, raw, hi, ALU.subtract).then_inc(shared[n].w_lo, 1)

            def rest_xt(n, b):
                dve.wait_ge(shared[n].x_hi, x_count(n, b))
                nc.vector.tensor_tensor(x_lo[:, :, :].rearrange("p k (r t) -> p r k t", r=BT),
                                        xt_in[:, :, :].rearrange("p r (k t) -> p r k t", k=KC),
                                        x_hi[:, :, :].rearrange("p k (r t) -> p r k t", r=BT), ALU.subtract
                                        ).then_inc(shared[n].x_lo, 1)

            def hiddens(n, b, ahead=0, between=None, front=0):
                f, chunks = shared[n], len(PARTS[n])
                for j in range(chunks):
                    if ahead and j + ahead < chunks:
                        split_shared(n, j + ahead)
                    if front:
                        front_slot(b, j, front)
                    hidden(f, b * chunks + j, j, P, BN, bank_h[2 * (j % 2) + 1][:, :], j % 2)
                    if between:
                        between(j)

            def row_sum(n, b, r):
                f, t = shared[n], b * BT + r
                if n == 1:
                    dve.wait_ge(picked_in[r % 2], 32 * (b * 2 + r // 2 + 1))
                    for k, done in enumerate((pick_half, picked_used)):
                        nc.vector.scalar_tensor_tensor(out=res[:, r, :], in0=picked[:, r % 2, k, :],
                                                       scalar=p_top[:, k, bass.ds(t, 1)],
                                                       in1=res[:, r, :], op0=ALU.mult, op1=ALU.add).then_inc(done, 1)
                        dve.wait_ge(done, t + 1)
                dve.wait_ge(f.o_full, t + 1)
                nc.vector.scalar_tensor_tensor(out=res[:, r, :], in0=bank_o[r % 2][:, :], scalar=s_gate[:, bass.ds(t, 1)],
                                               in1=res[:, r, :], op0=ALU.mult, op1=ALU.add).then_inc(f.o_kept, 1)

            def shared_tail(n, b, front=0):
                if n == 0 and not (isinstance(b, int) and b > FULL + 1):
                    dve.wait_ge(gate_ready, b + 1)
                dve.wait_ge(res_loaded[n], 16 * (b + 1))
                for r in range(BT):
                    if front and r < 3:
                        front_slot(b, len(PARTS[0]) + r, front)
                    row_sum(n, b, r)
                    if r == (2 if front == SLOTS else 0):
                        rest_xt(n, b + 1)

            def steps_of(at):
                return lambda j: at[j]() if j in at else None

            dve.wait_ge(shared[0].raw_loaded[0], 32)
            raw, hi, lo = next(shared_pieces(0, 0))
            nc.vector.tensor_copy(hi, raw).then_inc(first_w_hi, 1)
            dve.wait_ge(first_w_hi, 1)
            nc.vector.tensor_tensor(lo, raw, hi, ALU.subtract).then_inc(shared[0].w_lo, 1)
            for t0 in range(0, LEAD, 2):
                for t in (t0, t0 + 1):
                    dve.wait_ge(ft_done, t + 1)
                    nc.vector.tensor_copy(xt_in[:, t, :], lead_bank[t][:, :]).then_inc(fxt_ready, 1)
                for t in (t0, t0 + 1):
                    dve.wait_ge(lead_hi, t + 1)
                    c = slice(t * P, (t + 1) * P)
                    nc.vector.tensor_tensor(x_lo[:, :, c], xt_in[:, t, :].rearrange("p (k t) -> p k t", k=KC),
                                            x_hi[:, :, c], ALU.subtract).then_inc(lead_lo, 1)
            split_shared(0, 0, (1,))
            split_shared(0, 1, (0,))
            for t in range(2):
                front_logits(t, bank_h[2 + t])
            split_shared(0, 1, (1,))
            hiddens(0, 0, EARLY[0], front=SLOTS)
            shared_tail(0, 0, front=SLOTS)
            with dve.Fori(1, FULL) as b:
                hiddens(0, b, front=SLOTS)
                shared_tail(0, b, front=SLOTS)
            hiddens(0, FULL, front=LAST)
            shared_tail(0, FULL, front=LAST)
            dve.wait_ge(consts_in, 16)
            nc.vector.memset(ones_bf[:, :], 1.0)
            nc.vector.tensor_copy(before_bf[:, :], const("before"))
            nc.vector.tensor_copy(col_bf[:, :], const("col"))
            link(nc.vector.tensor_copy(ctile_bf[:, :], const("choice_tile")))
            hiddens(0, FULL + 1, between=steps_of({0: route_first, 1: route_second}))
            shared_tail(0, FULL + 1)
            route_weights()
            expert_starts()
            slot_bases()
            hiddens(0, FULL + 2, between=steps_of({0: choice_slots, 1: slot_places, 2: lambda: choice_ids(0),
                                                   3: lambda: choice_ids(1), 4: tile_experts}))
            shared_tail(0, FULL + 2)
            choice_ids(2)
            hiddens(0, FULL + 3, between=lambda j: choice_ids(j + 3) if j < 4 else None)
            shared_tail(0, FULL + 3)
            choice_ids(7)
            hiddens(0, BLOCKS - 1, between=steps_of({0: slot_tokens}))

            def split_w(i, u, part):
                pieces = list(expert_pieces(u))
                for k in part:
                    raw, hi, lo = pieces[k]
                    dve.wait_ge(ex.w_hi, PIECES * i + k + 1)
                    nc.vector.tensor_tensor(lo, raw, hi, ALU.subtract).then_inc(ex.w_lo, 1)

            def expert_hidden(i, j):
                fn = FCH[j][1]
                hidden(ex, 3 * i + j, j, fn, TS, bank_h[j][0:fn, TS:2 * TS], j)

            def whole_step(i, u, hidden_first=False, row_tiles=2):
                for j in range(3):
                    if hidden_first:
                        expert_hidden(i, j)
                    split_w(i + 1, 1 - u, (2 * j, 2 * j + 1))
                    if not hidden_first:
                        expert_hidden(i, j)
                if row_tiles == 1:
                    dve.wait_ge(ex.x_hi, 2 * (i + 2))
                    nc.vector.tensor_tensor(x_lo[:, :, TS:TS + P], bank_t[0][:, :].rearrange("p (k t) -> p k t", k=KC),
                                            x_hi[:, :, TS:TS + P], ALU.subtract).then_inc(ex.x_lo, 2)
                else:
                    for r in range(2):
                        rest_x(ex, 2 * (i + 1) + r, r)
                split_w(i + 1, 1 - u, (6,))

            def single_and_whole(i):
                split_w(i + 1, 1, (0,))
                for r in range(2):
                    rest_x(ex, 2 * (i + 1) + r, r)
                split_w(i + 1, 1, (1,))
                dve.wait_ge(ex.g_ready, 3 * (i + 1))
                dve.wait_ge(ex.h_full, 3 * (i + 1))
                nc.vector.tensor_tensor(h_sb[:, 0:F], bank_h[2][:, 0:F], g_sb[:, 0:F], ALU.mult).then_inc(ex.h_mul, 3)
                split_w(i + 1, 1, (2, 3))
                dve.wait_ge(ex.h_hi, 3 * (i + 1))
                for j in (slice(0, 2), slice(2, 3)):
                    fn = FCH[j.start][1]
                    nc.vector.tensor_tensor(h_lo[0:fn, 3 + j.start:3 + j.stop, 0:P],
                                            bank_h[3][0:fn, j.start * P:j.stop * P].rearrange("p (j t) -> p j t", t=P),
                                            h_hi[0:fn, 3 + j.start:3 + j.stop, 0:P], ALU.subtract
                                            ).then_inc(ex.h_lo, 2 - j.start // 2)
                split_w(i + 1, 1, range(KC, PIECES))
                for j in range(2):
                    expert_hidden(i + 1, j)
                split_w(i + 2, 0, (0, 1))
                expert_hidden(i + 1, 2)
                split_w(i + 2, 0, (2, 3))
                for r in range(2):
                    rest_x(ex, 2 * (i + 2) + r, r)
                split_w(i + 2, 0, range(KC, PIECES))

            dve.wait_ge(res_loaded[0], 16 * BLOCKS)
            for r in range(BT):
                split_w(0, 0, (r,))
                if r >= 2:
                    rest_x(ex, r - 2, r - 2)
                row_sum(0, BLOCKS - 1, r)
            split_w(0, 0, range(KC, PIECES))
            whole_step(0, 0, True)
            whole_step(1, 1, row_tiles=1)
            with dve.Fori(0, GROUPS) as g:
                single_and_whole(2 + 4 * g)
                whole_step(4 + 4 * g, 0)
                whole_step(5 + 4 * g, 1, row_tiles=1)
            single_and_whole(TAIL - 2)
            with dve.Fori(TAIL // 2, (XT - 1) // 2) as it:
                for u in range(2):
                    whole_step(2 * it + u, u)
            for j in range(3):
                if j < 2:
                    split_shared(1, j)
                expert_hidden(XT - 1, j)
            for k in range(KC):
                dve.wait_ge(shared[1].x_hi, k + 1)
                nc.vector.tensor_tensor(chunk(x_lo, k), xt_chunk(k), chunk(x_hi, k), ALU.subtract
                                        ).then_inc(shared[1].x_lo, 1)
            split_shared(1, 2)
            hiddens(1, 0, EARLY[1])
            shared_tail(1, 0)
            with dve.Fori(1, BLOCKS - 1) as b:
                hiddens(1, b)
                shared_tail(1, b)
            hiddens(1, BLOCKS - 1)
            dve.wait_ge(res_loaded[1], 16 * BLOCKS)
            for r in range(BT):
                row_sum(1, BLOCKS - 1, r)


def constants():
    import numpy as np
    c = {
        "ident": np.eye(P),
        "before": np.triu(np.ones((P, P)), 1),
        "rev": np.tile(np.repeat(E - np.arange(E), TILES), (P, 1)),
        "col": np.tile(np.arange(P), (P, 1)),
        "pidx": np.arange(P)[:, None],
        "choice_tile": np.tile(np.arange(CHOICES) % TILES, (P, 1)),
        "thr": np.tile(np.arange(THR) * TS, (P, 1)),
        "key": np.tile(np.array(KEYS), (P, 1)),
        "single_key": np.tile(HALVES - 1 - np.array(KEYS), (P, 1)),
    }
    return np.ascontiguousarray(np.concatenate([c[k] for k in CONST], axis=1).astype(np.float32))


def kernel(x, itok_B_0_7, L0_cond_weights, L0_ffn_gate_w, L0_ffn_expert_fc1, L0_ffn_expert_fc2, L0_ffn_expert_proj,
           L0_ffn_shared_fc1, L0_ffn_shared_fc2, L0_ffn_shared_proj, L0_ffn_shared_gate_w):
    import numpy as np
    import concourse.bacc as bacc
    from concourse import mybir as mb
    from concourse.bass_utils import run_bass_kernel_spmd

    gates = np.concatenate([np.asarray(L0_ffn_gate_w), np.asarray(L0_ffn_shared_gate_w)], axis=0)
    up = np.concatenate([np.asarray(L0_ffn_expert_fc1), np.asarray(L0_ffn_expert_fc2)], axis=1)
    sup = np.stack([np.asarray(L0_ffn_shared_fc1).reshape(SCH, P, C), np.asarray(L0_ffn_shared_fc2).reshape(SCH, P, C)], 1)
    arrays = {
        "x": np.asarray(x),
        "subj": np.asarray(itok_B_0_7).reshape(1, BATCH),
        "cond_w": np.asarray(L0_cond_weights),
        "gates": gates.T.reshape(KC, P, E + 1).transpose(1, 0, 2),
        "ew12": up.transpose(0, 2, 1).reshape(E, KC, P, 2 * F).transpose(0, 2, 1, 3).reshape(E, P, KC * 2 * F),
        "ewp": np.asarray(L0_ffn_expert_proj).transpose(0, 2, 1),
        "sw12": sup.transpose(0, 3, 1, 2).reshape(SCH, KC, P, 2 * P).transpose(0, 2, 1, 3).reshape(SCH, P, KC * 2 * P),
        "swp": np.asarray(L0_ffn_shared_proj).T.reshape(SCH, P, C),
        "consts": constants(),
    }
    nc = bacc.Bacc("TRN2", target_bir_lowering=False, num_devices=1)
    aps, sent = [], {}
    for name, a in arrays.items():
        a = np.ascontiguousarray(a)
        sent[name] = a
        aps.append(nc.dram_tensor(name, a.shape, mb.dt.from_np(a.dtype), kind="ExternalInput").ap())
    out = nc.dram_tensor("out", (BATCH, DOUT, C), mb.dt.float32, kind="ExternalOutput").ap()
    build_program(nc, *aps, out)
    r = run_bass_kernel_spmd(nc, [sent], core_ids=[0])
    return r.results[0]["out"]
```
